# Optimizing a Trainium2 kernel written in Bass

```python
import numpy as np
import jax
import jax.numpy as jnp

def _softmax(x, axis=-1):
    return jax.nn.softmax(x, axis=axis)

def _gelu(x):
    return jax.nn.gelu(x, approximate=True)

def _silu(x):
    return jax.nn.silu(x)

def _sigmoid(x):
    return jax.nn.sigmoid(x)

def _layernorm(x, axis=-1, eps=1e-05):
    m = jnp.mean(x, axis=axis, keepdims=True)
    v = jnp.var(x, axis=axis, keepdims=True)
    return (x - m) / jnp.sqrt(v + eps)

def _scatter_add(tgt, idx, src, axis=0):
    return tgt.at[idx].add(src)

def _segment_sum(src, seg, n):
    return jax.ops.segment_sum(src, seg, n)
kernel_name = 'mk_flamingo_gated_d1_seqx_r4_21e41c'

def setup_inputs(seed: int=0):
    np.random.seed(seed)
    _w = jnp.asarray

    def _rec_inputs():
        import jax
        import jax.numpy as jnp
        _rk = jax.random.key(seed)
        x = -0.0005207 + 1.001 * jax.random.normal(jax.random.fold_in(_rk, 1), (8, 256, 512), jnp.float32)
        _lenS = 256 - jax.random.randint(jax.random.fold_in(_rk, 7), (8,), 0, max(1, 256 // 4) + 1, jnp.int32)
        _lenS2 = 256 - jax.random.randint(jax.random.fold_in(_rk, 8), (8,), 0, max(1, 256 // 4) + 1, jnp.int32)
        _ctx_2048P = jax.random.normal(jax.random.fold_in(_rk, 11), (8, 16, 512), jnp.float32)
        _ctx_2048c = jax.random.dirichlet(jax.random.fold_in(_rk, 511), 0.3 * jnp.ones((16,), jnp.float32), (8, 256))
        _ctx_2048t = jnp.einsum('bsk,bkd->bsd', _ctx_2048c, _ctx_2048P)
        _ctx_2048t = _ctx_2048t * jax.lax.rsqrt(jnp.mean(jnp.square(_ctx_2048t)) + 1e-12) * 0.953939
        ctx_2048 = -0.000514642 + 1.00011 * (_ctx_2048t + 0.3 * jax.random.normal(jax.random.fold_in(_rk, 611), (8, 256, 512), jnp.float32))
        _g = jax.random.normal(jax.random.fold_in(_rk, 9001), (2, 1), jnp.float32)
        _g = jnp.sign(_g) * jnp.maximum(jnp.abs(_g), 1.0) + (_g == 0) * 1.0
        g_xattn = _g[0]
        g_ffn = _g[1]
        return (x, ctx_2048, g_xattn, g_ffn)
    x, ctx_2048, g_xattn, g_ffn = _rec_inputs()

    def _L0_xattn_setup():
        import jax, jax.numpy as jnp
        import numpy as np
        from math import sqrt
        key = jax.random.key(seed)
        kq, kk, kv = jax.random.split(key, 3)
        B, D, N = (8, 128, 512)
        Q = jax.random.normal(kq, (B, D, N), dtype=jnp.float32)
        K = jax.random.normal(kk, (B, D, N), dtype=jnp.float32)
        V = jax.random.normal(kv, (B, D, N), dtype=jnp.float32)
        return {'Q': Q, 'K': K, 'V': V}
    _L0_xattn_all = _L0_xattn_setup()
    _L0_xattn_in = {k: v for k, v in _L0_xattn_all.items() if k in ()}
    del _L0_xattn_all

    def _L0_ffn_setup():
        import jax, jax.numpy as jnp
        import numpy as np
        ALPHA = 1.702
        LIMIT = 7.0
        EPS = 1e-05
        TOP_K = 4
        key = jax.random.key(seed)
        ks = jax.random.split(key, 8)
        B, S, H, I, E = (2, 128, 512, 512, 16)
        return {'x': jax.random.normal(ks[0], (B, S, H), jnp.float32), 'norm_w': jnp.ones((H,), jnp.float32), 'gate_w': jax.random.normal(ks[1], (E, H), jnp.float32) * 0.02, 'gate_b': jax.random.normal(ks[2], (E,), jnp.float32) * 0.02, 'w1': jax.random.normal(ks[3], (E, 2 * I, H), jnp.float32) * 0.02, 'b1': jax.random.normal(ks[4], (E, 2 * I), jnp.float32) * 0.02, 'w2': jax.random.normal(ks[5], (E, H, I), jnp.float32) * 0.02, 'b2': jax.random.normal(ks[6], (E, H), jnp.float32) * 0.02}
    _L0_ffn_all = _L0_ffn_setup()
    _L0_ffn_in = {k: v for k, v in _L0_ffn_all.items() if k in ('norm_w', 'gate_w', 'gate_b', 'w1', 'b1', 'w2', 'b2')}
    del _L0_ffn_all
    return {'x': x, 'ctx_2048': ctx_2048, 'g_xattn': g_xattn, 'g_ffn': g_ffn, 'L0_ffn_norm_w': _L0_ffn_in['norm_w'], 'L0_ffn_gate_w': _L0_ffn_in['gate_w'], 'L0_ffn_gate_b': _L0_ffn_in['gate_b'], 'L0_ffn_w1': _L0_ffn_in['w1'], 'L0_ffn_b1': _L0_ffn_in['b1'], 'L0_ffn_w2': _L0_ffn_in['w2'], 'L0_ffn_b2': _L0_ffn_in['b2']}

def reference(x, ctx_2048, g_xattn, g_ffn, L0_ffn_norm_w, L0_ffn_gate_w, L0_ffn_gate_b, L0_ffn_w1, L0_ffn_b1, L0_ffn_w2, L0_ffn_b2):
    import jax
    import jax.numpy as jnp

    def _L0_xattn_ref(Q, K, V):
        import jax, jax.numpy as jnp
        import numpy as np
        from math import sqrt
        dk = Q.shape[1]
        x = jnp.einsum('bdn,bdm->bnm', Q, K) / sqrt(dk)
        score = jax.nn.sigmoid(x)
        out = jnp.einsum('bvn,bnm->bvm', V, score)
        return out

    def _L0_ffn_ref(x, norm_w, gate_w, gate_b, w1, b1, w2, b2):
        import jax, jax.numpy as jnp
        import numpy as np
        ALPHA = 1.702
        LIMIT = 7.0
        EPS = 1e-05
        TOP_K = 4
        B, S, H = x.shape
        M = B * S
        E = gate_w.shape[0]
        xf = x.reshape(M, H)
        t = xf * jax.lax.rsqrt(jnp.mean(xf * xf, axis=-1, keepdims=True) + EPS) * norm_w
        logits = t @ gate_w.T + gate_b
        vals, idx = jax.lax.top_k(logits, TOP_K)
        gates_k = jax.nn.softmax(vals, axis=-1)
        G = jnp.zeros((M, E), x.dtype).at[jnp.arange(M)[:, None], idx].set(gates_k)
        h = jnp.einsum('mh,eoh->emo', t, w1) + b1[:, None, :]
        a = jnp.minimum(h[..., ::2], LIMIT)
        b = jnp.clip(h[..., 1::2], -LIMIT, LIMIT)
        act = a * jax.nn.sigmoid(ALPHA * a) * (b + 1.0)
        y = jnp.einsum('emi,edi->emd', act, w2) + b2[:, None, :]
        delta = jnp.einsum('me,emd->md', G, y)
        return x + delta.reshape(B, S, H)
    x = x + jnp.tanh(g_xattn[0]) * _L0_xattn_ref(_layernorm(x, axis=-1), ctx_2048, ctx_2048)
    x = x + jnp.tanh(g_ffn[0]) * _L0_ffn_ref(_layernorm(x, axis=-1), L0_ffn_norm_w, L0_ffn_gate_w, L0_ffn_gate_b, L0_ffn_w1, L0_ffn_b1, L0_ffn_w2, L0_ffn_b2)
    return x

_drawn_inputs = setup_inputs


def setup_inputs(seed=0):
    import zlib

    import numpy as np

    out = dict(_drawn_inputs(seed))
    spreads = {'L0_ffn_norm_w': (1.0, 0.6)}
    factors = {'L0_ffn_gate_w': 8.0,
     'L0_ffn_gate_b': 8.0,
     'L0_ffn_w1': 8.0,
     'L0_ffn_b1': 8.0,
     'L0_ffn_w2': 8.0,
     'L0_ffn_b2': 64.0}
    for name, (base, spread) in spreads.items():
        noise = np.random.default_rng([zlib.crc32(name.encode()), seed]).standard_normal(out[name].shape)
        drawn = base * np.exp(spread * noise) if base else spread * noise
        out[name] = jnp.asarray(drawn.astype(out[name].dtype))
    for name, factor in factors.items():
        out[name] = (out[name] * factor).astype(out[name].dtype)
    return out
```

```python
from contextlib import ExitStack

import numpy as np

import concourse.bass as bass
from concourse import mybir

ALU = mybir.AluOpType
AF = mybir.ActivationFunctionType
F32 = mybir.dt.float32
F32R = mybir.dt.float32r
BF16 = mybir.dt.bfloat16
I32 = mybir.dt.int32
U32 = mybir.dt.uint32
AX = mybir.AxisListType.X

B = 8
S = 256
H = 512
E = 16
K = 4
M = B * S
NI = M // 128
NT = M * K // 128 + E - 1
ENDS = (72, 75)
VT = E * NI
NTP = 80
ROW = H + E
WS = 4 * 1536
NCH = 4
CW = 1536
POOL_HOTS = ()
EPS = 1e-5
LIMIT = 7.0
ALPHA = 1.702

C_ID = 0
C_SU = 128
C_IOTA = 256
C_TOK = 512
C_SEL = 528
C_CNT = 579
C_STEP = 611
C_PAD = 612
C_N = 613


def shape_constants():
    c = np.zeros((128, C_N), np.float32)
    p = np.arange(128)
    c[:, C_ID:C_ID + 128] = np.eye(128)
    c[:, C_SU:C_SU + 128] = p[:, None] < p[None, :]
    c[:, C_IOTA:C_IOTA + 256] = np.arange(256)
    c[:, C_TOK:C_TOK + NI] = 128 * np.arange(NI) + p[:, None] + 1
    sel = np.zeros((128, 3, E + 1), np.float32)
    for h in range(2):
        sel[p, h, 8 * h + p // 16] = 1
        sel[:, h, E] = p % 16
    for q in range(128):
        if q < E - 1:
            sel[q, 2, q + 1] = 1
        else:
            sel[q, 2, E] = 1000
    c[:, C_SEL:C_SEL + 51] = sel.reshape(128, 51)
    q = p[:E - 1]
    cnt = np.zeros((128, 2, E), np.float32)
    cnt[q, 0, q] = 1
    cnt[q, 1, q + 1] = 1
    cnt[q, 1, q] = -1
    c[:, C_CNT:C_CNT + 32] = cnt.reshape(128, 32)
    c[:E - 1, C_STEP] = (q + 1) % 3 - q % 3
    c[:, C_PAD] = M + 1 + p
    return c


class Line:

    def __init__(self, name, sem):
        self.name, self.sem, self.n, self.items, self.seen = name, sem, 0, [], {}

    def put(self, fn, *waits, on=None):
        if on is not None:
            on[1] += 1
            self._push(fn, waits, (on[0], 1))
            return (on[0], on[1])
        self.n += 1
        self._push(fn, waits, (self.sem, 1))
        return (self.sem, self.n)

    def dma(self, fn, chan, *waits):
        chan[1] += 16
        self._push(fn, waits, (chan[0], 16))
        return (chan[0], chan[1])

    def only(self, cond):
        self.items.append((cond, None, "if"))

    def close(self):
        self.items.append((None, None, "end"))

    def run(self, fn, *waits):
        self._push(fn, waits, None)

    def _push(self, fn, waits, inc):
        need = []
        for sem, val in waits:
            if self.seen.get(sem.name, 0) < val:
                self.seen[sem.name] = val
                need.append((sem, val))
        self.items.append((fn, need, inc))

    def emit(self, eng):
        inside = []
        for fn, need, inc in self.items:
            if inc == "if":
                inside.append(ExitStack())
                inside[-1].enter_context(eng.If(fn(eng)))
            elif inc == "end":
                inside.pop().close()
            else:
                for sem, val in need:
                    eng.wait_ge(sem, val)
                ins = fn(eng)
                if inc is not None:
                    ins.then_inc(*inc)


def build(nc, x, ctx, ctxT, gx, gf, nw, gw, gb, wts, bias, cst, out):
    with ExitStack() as es:
        rows = nc.dram_tensor("rows", (M, ROW), F32, kind="Internal").ap()

        top = [16512]

        def at(name, shape, dt, offset):
            return nc.alloc_sbuf_tensor_at(name, shape, dt, offset=offset)

        def sb(name, shape, dt=F32):
            n = int(np.prod(shape[1:])) * mybir.dt.size(dt)
            t = at(name, shape, dt, top[0])
            top[0] += (n + 31) // 32 * 32
            return t

        HI = top[0]
        RAW = HI + 12 * WS
        BIAS = RAW + 12 * WS
        REST = BIAS + 12 * CW
        Wh = at("Wh", [128, 3, WS], F32R, HI)
        Wf = at("Wf", [128, 3, WS], F32, RAW)
        Wl = at("Wl", [128, 3, WS], F32R, RAW)
        Bs = at("Bs", [128, 3, CW], F32, BIAS)

        top[0] = REST
        C = sb("C", [128, C_N])
        te = sb("te", [128, 5, NTP], I32)
        src = sb("src", [128, NTP], I32)
        dst = sb("dst", [128, NTP], I32)
        Ei = sb("Ei", [128, E], I32)
        gcol = [sb(f"gcol{i}", [128, 1]) for i in range(4)]
        ones = sb("ones", [128, 128], BF16)
        stepb = sb("stepb", [128, 128], BF16)
        cntb = sb("cntb", [128, 2, 128], BF16)
        Ni = sb("Ni", [128, E], I32)
        Ti = sb("Ti", [128, E], I32)
        Tf = sb("Tf", [128, E])
        Ee = sb("Ee", [128, E])
        Tx = sb("Tx", [128, E + 1])
        us = sb("us", [128, 3, E + 1])
        uu = sb("uu", [128, 3])
        ut = sb("ut", [128, 2, E])
        un = sb("un", [128, 2])
        Sm = sb("Sm", [128, 2, NTP])
        cm = sb("cm", [128, NTP], BF16)
        tab = sb("tab", [128, VT])
        tabT = sb("tabT", [128, 2, 128])
        iv = sb("iv", [128, NTP])
        j4 = sb("j4", [128, NTP])
        fl = [sb(f"fl{i}", [128, NTP]) for i in range(NCH)]
        Tm = sb("Tm", [128, 1])
        tail = top[0]

        xg = [sb(f"xg{i}", [128, ROW]) for i in range(4)]
        xTh = [sb(f"xTh{i}", [128, 4, 128], F32R) for i in range(2)]
        xTl = [sb(f"xTl{i}", [128, 4, 128], F32R) for i in range(2)]
        av_ = sb("av_", [128, H])
        sg = sb("sg", [128, H])
        bv_ = sb("bv_", [128, H])
        hh = sb("hh", [128, H])
        aTh = sb("aTh", [128, 4, 128], F32R)
        aTl = sb("aTl", [128, 4, 128], F32R)
        ys = [sb(f"ys{i}", [128, H]) for i in range(3)]
        small = top[0]

        top[0] = RAW + 4 * WS
        Sc = [sb(f"Sc{i}", [128, 4, H]) for i in range(2)]
        Qt = [sb(f"Qt{i}", [128, 2, H]) for i in range(2)]
        assert top[0] <= RAW + 8 * WS
        Kt = [sb(f"Kt{i}", [128, 2, H]) for i in range(2)]
        Vt = [sb(f"Vt{i}", [128, 4, S]) for i in range(2)]
        OV = sb("OV", [128, 2 * K, VT], F32R)
        assert top[0] <= BIAS
        top[0] = BIAS + 8 * CW
        OL = sb("OL", [128, 2 * K, 128], F32R)
        assert top[0] <= REST
        top[0] = HI + 4 * WS
        X = [sb(f"X{i}", [128, 2, H]) for i in range(3)]
        x1 = [sb(f"x1_{i}", [128, 2, H]) for i in range(2)]
        tt = [sb(f"tt{i}", [128, 2, ROW]) for i in range(2)]
        base = [sb(f"base{i}", [128, 2, H]) for i in range(2)]
        tTs = [sb(f"tTs{i}", [128, 4, 128]) for i in range(2)]
        nwb = sb("nwb", [128, H])
        zero = sb("zero", [128, H])
        assert top[0] <= RAW

        top[0] = tail
        gwT = sb("gwT", [128, 4, E])
        gbb = sb("gbb", [128, E])
        gg = sb("gg", [128, 2])
        tg = sb("tg", [128, 2])
        tn = sb("tn", [128, 2])
        mh = sb("mh", [128, 4])
        SUb = sb("SUb", [128, 128], BF16)
        Mac = sb("Mac", [128, B + 1, E], BF16)
        st = sb("st", [128, 2, 6])
        mv = [sb(f"mv{i}", [128, 2, 2]) for i in range(2)]
        ve = [sb(f"ve{i}", [128, 2]) for i in range(2)]
        rs = [sb(f"rs{i}", [128, 2]) for i in range(2)]
        nb = [sb(f"nb{i}", [128, 2]) for i in range(2)]
        st1 = sb("st1", [128, 2, 6])
        mv1 = [sb(f"mv1_{i}", [128, 2, 2]) for i in range(2)]
        ve1 = [sb(f"ve1_{i}", [128, 2, 2]) for i in range(2)]
        rs1 = [sb(f"rs1_{i}", [128, 2, 2]) for i in range(2)]
        c1 = [sb(f"c1_{i}", [128, 2]) for i in range(2)]
        mc = [sb(f"mc_{i}", [128, 2]) for i in range(2)]
        nt = [sb(f"nt_{i}", [128, 2]) for i in range(2)]
        Lg = sb("Lg", [128, 2, E])
        mx = sb("mx", [128, 2, 8])
        ix = sb("ix", [128, 2, 8], U32)
        dd = sb("dd", [128, 2, K])
        s1 = sb("s1", [128, 2, K])
        s2 = sb("s2", [128, 2, K])
        ex = sb("ex", [128, 2, K])
        zz = sb("zz", [128, 2])
        gk = sb("gk", [128, 2, K])
        idf = [sb(f"idf{i}", [128, 2, K]) for i in range(2)]
        oh = [sb(f"oh{i}", [128, 2, K, E]) for i in range(2)]
        og = sb("og", [128, 2, K, E])
        op = sb("op", [128, 2, K, E])
        mk = [sb(f"mk{i}", [128, 2, E], BF16) for i in range(2)]
        ms = sb("ms", [128, E], BF16)
        rr = sb("rr", [128, 2 * K])
        rh = sb("rh", [128, 2 * K], I32)
        vt = sb("vt", [128, 2 * K])
        lof = sb("lof", [128, 2 * K])
        assert max(top[0], small) <= 229368, (top[0], small)

        ps = [es.enter_context(nc.psum_tensor(f"ps{i}", [128, 512], F32)) for i in range(8)]

        sem = lambda n: es.enter_context(nc.semaphore(n))
        chans = []

        def chan(n):
            chans.append([sem(n), 0])
            return chans[-1]

        s_raw = chan("s_raw")
        s_hi = chan("s_hi")
        s_lo = chan("s_lo")
        s_yb = chan("s_yb")
        PE, ACT, DVE, POOL, SP = [Line(n, sem(n)) for n in ("pe", "act", "dve", "pool", "sp")]
        d_c = chan("d_c")
        d_c2 = chan("d_c2")
        d_x = [chan(f"d_x{i}") for i in range(3)]
        d_k = [chan(f"d_k{i}") for i in range(2)]
        d_v = [chan(f"d_v{i}") for i in range(2)]
        d_o = [chan(f"d_o{i}") for i in range(2)]
        d_r = [chan(f"d_r{i}") for i in range(2)]
        d_z = chan("d_z")
        d_w = [chan(f"d_w{i}") for i in range(3)]
        d_g = [chan(f"d_g{i}") for i in range(4)]
        d_s = chan("d_s")

        xb = x.rearrange("(b j p) h -> b p j h", j=2, p=128)
        cb = ctx.rearrange("b (j p) h -> b p j h", p=128)
        ob = out[0:M, :].rearrange("(b j p) h -> b p j h", j=2, p=128)
        rb = rows.rearrange("(b j p) h -> b p j h", j=2, p=128)

        idm = C[:, C_ID:C_ID + 128]
        iota = lambda n: C[:, C_IOTA:C_IOTA + n]
        T = {}
        was = lambda *key: [T[key]] if key in T else []

        def load_x(b):
            T["lx", b] = SP.dma(lambda e: e.dma_start(X[b % 3][:], xb[b]), d_x[b % 3], *was("x1", b - 3))

        def load_k(b):
            T["lk", b] = SP.dma(lambda e: e.dma_start(Kt[b % 2][:], cb[b]), d_k[b % 2], *was("qk", b - 2))

        def load_v(b):
            T["lv", b] = SP.dma(lambda e: e.dma_start(Vt[b % 2][:], ctxT[b]), d_v[b % 2], *was("av", b - 2))

        def ln(b):
            i = b % 2
            for j in range(2):
                t = DVE.put(lambda e, j=j: e.bn_stats(st[:, j, :], X[b % 3][:, j, :]), T["lx", b])
                yield
            for j in range(2):
                t = DVE.put(lambda e, j=j: e.bn_aggr(mv[i][:, j, :], st[:, j, :]), t, *was("nq", b - 2))
                yield
            t = DVE.put(lambda e: e.tensor_scalar(ve[i][:], mv[i][:, :, 1], EPS, None, op0=ALU.add), t)
            p = POOL.put(lambda e: e.tensor_tensor(rs[i][:], ve[i][:], mh[:, 0:2], ALU.pow), t)
            yield
            T["nb", b] = DVE.put(lambda e: e.scalar_tensor_tensor(nb[i][:], mv[i][:, :, 0], -1.0, rs[i][:], ALU.mult, ALU.mult), p)
            yield

        def norm_q(b):
            i = b % 2
            for j in range(2):
                T["q", b] = T["nq", b] = ACT.put(lambda e, j=j: e.activation(
                    Qt[i][:, j, :], X[b % 3][:, j, :], AF.Identity, bias=nb[i][:, j:j + 1], scale=rs[i][:, j:j + 1]),
                    T["nb", b], *was("qk", b - 2))

        def qk(b, cs):
            i = b % 2
            for c in cs:
                def mm(e, c=c):
                    for k in range(2):
                        m = e.matmul(ps[c % 2][:], Qt[i][:, k, 128 * c:128 * c + 128], Kt[i][:, k, :], start=(k == 0), stop=(k == 1))
                    return m
                T["qk", b] = PE.put(mm, T["q", b], T["lk", b], *was("sg", c % 2))
                T["sg", c % 2] = T["sc", b] = ACT.put(
                    lambda e, c=c: e.activation(Sc[i][:, c, :], ps[c % 2][:], AF.Sigmoid, scale=1.0 / 16.0), T["qk", b], *was("av", b - 2))

        def av(b):
            i = b % 2
            for j in range(2):
                def mm(e, j=j):
                    for c in range(4):
                        m = e.matmul(ps[2 + j][:], Vt[i][:, c, 128 * j:128 * j + 128], Sc[i][:, c, :], start=(c == 0), stop=(c == 3))
                    return m
                T["av", b] = T["avj", j] = PE.put(mm, T["sc", b], T["lv", b], *was("x1j", j))

        def add_x(b):
            for j in range(2):
                T["x1j", j] = T["x1", b] = DVE.put(
                    lambda e, j=j: e.scalar_tensor_tensor(x1[b % 2][:, j, :], ps[2 + j][:], tg[:, 0:1], X[b % 3][:, j, :], ALU.mult, ALU.add),
                    T["avj", j], T["tg"], *was("base", b - 2), *was("tn", b - 2))

        def ffn_in(b):
            i = b % 2
            for j in range(2):
                t = DVE.put(lambda e, j=j: e.bn_stats(st1[:, j, :], x1[b % 2][:, j, :]), T["x1", b])
                yield
            for j in range(2):
                t = DVE.put(lambda e, j=j: e.bn_aggr(mv1[i][:, j, :], st1[:, j, :]), t, *was("base", b - 2))
                yield
            t0 = DVE.put(lambda e: e.tensor_scalar(ve1[i][:, 0, :], mv1[i][:, :, 1], EPS, None, op0=ALU.add), t)
            yield
            t = DVE.put(lambda e: e.scalar_tensor_tensor(ve1[i][:, 1, :], ve1[i][:, 0, :], EPS, mv1[i][:, :, 1], ALU.mult, ALU.add), t0)
            p = POOL.put(lambda e: e.tensor_tensor(rs1[i][:].rearrange("p a j -> p (a j)"), ve1[i][:].rearrange("p a j -> p (a j)"), mh[:], ALU.pow), t)
            yield
            T["nt", b] = DVE.put(lambda e: e.scalar_tensor_tensor(nt[i][:], mv1[i][:, :, 0], -1.0, rs1[i][:, 1, :], ALU.mult, ALU.mult), p)
            yield
            DVE.put(lambda e: e.tensor_scalar(c1[i][:], rs1[i][:, 0, :], tg[:, 1:2], 1.0, op0=ALU.mult, op1=ALU.add), p)
            yield
            T["mc", b] = DVE.put(lambda e: e.scalar_tensor_tensor(mc[i][:], rs1[i][:, 0, :], tn[:, 1:2], mv1[i][:, :, 0], ALU.mult, ALU.mult), p)
            yield

        def norm_t(b):
            i = b % 2
            for j in range(2):
                T["tn", b] = ACT.put(lambda e, j=j: e.activation(tt[i][:, j, 0:H], x1[b % 2][:, j, :], AF.Identity, bias=nt[i][:, j:j + 1],
                                                                 scale=rs1[i][:, 1, j:j + 1]), T["nt", b], *was("st_row", b - 2))
            for j in range(2):
                T["t", b] = POOL.put(lambda e, j=j: e.tensor_tensor(tt[i][:, j, 0:H], tt[i][:, j, 0:H], nwb[:], ALU.mult), T["tn", b])
            for j in range(2):
                T["base", b] = POOL.put(lambda e, j=j: e.tensor_scalar(base[i][:, j, :], x1[b % 2][:, j, :], c1[i][:, j:j + 1],
                                                                      mc[i][:, j:j + 1], op0=ALU.mult, op1=ALU.add),
                                        T["mc", b], *was("st_base", b - 2))
            T["st_base", b] = SP.dma(lambda e: e.dma_start(ob[b], base[i][:]), d_o[i], T["base", b])

        def logits(b):
            i = b % 2
            for j in range(2):
                def tr(e, j=j):
                    for c in range(4):
                        m = e.transpose(ps[4 + j][:, 128 * c:128 * c + 128], tt[i][:, j, 128 * c:128 * c + 128], idm)
                    return m
                t = PE.put(tr, T["t", b], *was("tTc", j))
                T["tTc", j] = ACT.put(lambda e, j=j: e.copy(tTs[j][:], ps[4 + j][:].rearrange("p (c t) -> p c t", c=4)), t, *was("lgm", j))
            for j in range(2):
                def mm(e, j=j):
                    for c in range(4):
                        m = e.matmul(ps[6][:, 16 * j:16 * j + 16], tTs[j][:, c, :], gwT[:, c, :], start=(c == 0), stop=(c == 3))
                    return m
                T["lgm", j] = T["lg", b] = PE.put(mm, T["tTc", j], *was("lgr"))

        def choose(b):
            i = b % 2
            t = T[("lgr",)] = DVE.put(lambda e: e.tensor_tensor(Lg[:], ps[6][:, 0:32].rearrange("p (j e) -> p j e", j=2),
                                                               gbb[:].unsqueeze(1).broadcast_to((128, 2, E)), ALU.add), T["lg", b])
            yield
            for j in range(2):
                t2 = DVE.put(lambda e, j=j: e.max(mx[:, j, :], Lg[:, j, :]), t)
                yield
            td = DVE.put(lambda e: e.tensor_tensor(dd[:], mx[:, :, 0:K], mx[:, :, 0:1].broadcast_to((128, 2, K)), ALU.subtract), t2)
            ACT.put(lambda e: e.activation(s1[:], dd[:], AF.Sigmoid), td)
            ts = ACT.put(lambda e: e.activation(s2[:], dd[:], AF.Sigmoid, scale=-1.0), td)
            yield
            for j in range(2):
                t2 = DVE.put(lambda e, j=j: e.max_index(ix[:, j, :], mx[:, j, :], Lg[:, j, :]), t2)
                yield
            t = DVE.put(lambda e: e.tensor_copy(idf[i][:], ix[:, :, 0:K]), t2)
            yield
            to = DVE.put(lambda e: e.tensor_tensor(
                oh[i][:].rearrange("p j k e -> p (j k) e"), idf[i][:].rearrange("p j k -> p (j k)").unsqueeze(2).broadcast_to((128, 2 * K, E)),
                iota(E).unsqueeze(1).broadcast_to((128, 2 * K, E)), ALU.is_equal), t)
            yield

            def red(e):
                with nc.allow_low_precision(reason="counts up to 4"):
                    return e.tensor_reduce(mk[i][:], oh[i][:].rearrange("p j k e -> p j e k"), AX, ALU.add)

            t = T["mk", b] = DVE.put(red, to, *was("pm", b - 2))
            p = POOL.put(lambda e: e.tensor_tensor(ms[:], mk[i][:, 0, :], mk[i][:, 1, :], ALU.add), t)
            T["mac", b + 1] = POOL.put(lambda e: e.tensor_tensor(Mac[:, b + 1, :], Mac[:, b, :], ms[:], ALU.add), p)
            yield
            t = DVE.put(lambda e: e.reciprocal(s2[:], s2[:]), ts)
            yield
            t = DVE.put(lambda e: e.tensor_tensor(ex[:], s1[:], s2[:], ALU.mult), t)
            yield
            t = DVE.put(lambda e: e.tensor_reduce(zz[:], ex[:], AX, ALU.add), t)
            yield
            t = DVE.put(lambda e: e.reciprocal(zz[:], zz[:]), t)
            yield
            t = DVE.put(lambda e: e.scalar_tensor_tensor(gk[:], ex[:], tg[:, 1:2], zz[:].unsqueeze(2).broadcast_to((128, 2, K)),
                                                         ALU.mult, ALU.mult), t)
            yield
            t = DVE.put(lambda e: e.tensor_tensor(
                og[:].rearrange("p j k e -> p (j k) e"), oh[i][:].rearrange("p j k e -> p (j k) e"),
                gk[:].rearrange("p j k -> p (j k)").unsqueeze(2).broadcast_to((128, 2 * K, E)), ALU.mult), t)
            yield
            t = DVE.put(lambda e: e.tensor_reduce(tt[i][:, :, H:ROW], og[:].rearrange("p j k e -> p j e k"), AX, ALU.add), t,
                        *was("st_row", b - 2))
            T["st_row", b] = SP.dma(lambda e: e.dma_start(rb[b], tt[i][:]), d_r[i], t, T["t", b])
            yield

        def before(b):
            i = b % 2

            def mm(e):
                e.matmul(ps[6][:, 32:48], SUb[:], mk[i][:, 0, :], start=True, stop=False)
                e.matmul(ps[6][:, 32:48], ones[:], Mac[:, b, :], start=False, stop=True)
                e.matmul(ps[6][:, 48:64], SUb[:], mk[i][:, 1, :], start=True, stop=False)
                e.matmul(ps[6][:, 48:64], ones[:], Mac[:, b, :], start=False, stop=False)
                return e.matmul(ps[6][:, 48:64], ones[:], mk[i][:, 0, :], start=False, stop=True)

            T["pm", b] = PE.put(mm, T["mk", b], T["mac", b], T["consts"], *was("prr"))

        def rank(b):
            i = b % 2
            t = T[("prr",)] = DVE.put(lambda e: e.tensor_tensor(
                op[:], oh[i][:], ps[6][:, 32:64].rearrange("p (j e) -> p j e", j=2).unsqueeze(2).broadcast_to((128, 2, K, E)), ALU.mult),
                T["pm", b])
            yield
            tr = DVE.put(lambda e: e.tensor_reduce(rr[:], op[:].rearrange("p j k e -> p (j k) e"), AX, ALU.add), t)
            yield
            th = DVE.put(lambda e: e.tensor_scalar(rh[:], rr[:], 1.0 / 128, -127.0 / 256, op0=ALU.mult, op1=ALU.add), tr)
            yield
            T["vt", b] = DVE.put(lambda e: e.scalar_tensor_tensor(vt[:], idf[i][:].rearrange("p j k -> p (j k)"), float(NI), rh[:],
                                                                  ALU.mult, ALU.add), th, *was("ov", b - 1))
            yield
            T["lo", b] = DVE.put(lambda e: e.scalar_tensor_tensor(lof[:], rh[:], -128.0, rr[:], ALU.mult, ALU.add), th)
            yield

        def one_hots(b):
            for q in range(2 * K):
                T["ol", b] = DVE.put(lambda e, q=q: e.tensor_scalar(OL[:, q, :], iota(128), lof[:, q:q + 1], None, op0=ALU.is_equal),
                                     T["lo", b], *was("tb", b - 1))
                yield
                n = 2 * b + q // K
                eng = POOL if q in POOL_HOTS else DVE
                T["ov" + eng.name, b] = eng.put(lambda e, q=q, n=n: e.tensor_scalar(
                    OV[:, q, :], iota(VT), vt[:, q:q + 1], C[:, C_TOK + n:C_TOK + n + 1], op0=ALU.is_equal, op1=ALU.mult),
                    T["vt", b], *was("tb", b - 1))
                yield
            T["ov", b] = T["ovpool", b] if POOL_HOTS else T["ovdve", b]

        def table(b):
            def mm(e):
                for q in range(2 * K):
                    m = e.matmul(ps[7][:, 0:VT], OL[:, q, :], OV[:, q, :], start=(b == 0 and q == 0), stop=(b == B - 1 and q == 2 * K - 1))
                return m
            T["tb", b] = PE.put(mm, T["ol", b], T["ovdve", b], T["ov", b])

        def load_w(e_, *w):
            s_ = e_ % 3
            SP.dma(lambda e: e.dma_start(Wf[:, s_, :], wts[e_]), d_w[s_], *w)
            SP.dma(lambda e: e.dma_start(Bs[:, s_, :], bias[e_:e_ + 1, :].partition_broadcast(128)), d_w[s_])

        def landed(e_):
            SP.run(lambda e: e.wait_ge(d_w[e_ % 3][0], 32 * (e_ // 3 + 1)))
            SP.run(lambda e: e.sem_inc(s_raw[0], 1))

        SP.dma(lambda e: e.dma_start(C[:], cst), d_c)
        SP.dma(lambda e: e.dma_start(gg[:, 0:1], gx.partition_broadcast(128)), d_c)
        T["ld"] = SP.dma(lambda e: e.dma_start(gg[:, 1:2], gf.partition_broadcast(128)), d_c)
        load_x(0)
        load_k(0)
        load_v(0)
        SP.dma(lambda e: e.dma_start(nwb[:], nw.partition_broadcast(128)), d_c2)
        SP.dma(lambda e: e.dma_start(gwT[:], gw), d_c2)
        T["ld2"] = SP.dma(lambda e: e.dma_start(gbb[:], gb.partition_broadcast(128)), d_c2)
        load_x(1)
        load_k(1)
        load_v(1)
        load_x(2)

        t = ACT.put(lambda e: e.activation(tg[:], gg[:], AF.Tanh), T["ld"])
        T["tg"] = ACT.put(lambda e: e.activation(tn[:], gg[:], AF.Tanh, scale=-1.0), T["ld"])
        T["mh"] = POOL.put(lambda e: e.memset(mh[:], -0.5))
        DVE.put(lambda e: e.memset(ones[:], 1.0))
        DVE.put(lambda e: e.memset(Mac[:, 0, :], 0.0))
        DVE.put(lambda e: e.memset(Tx[:, E:E + 1], 1.0))
        t = DVE.put(lambda e: e.memset(zero[:], 0.0))
        T["zero"] = SP.dma(lambda e: e.dma_start(out[M:M + 128, :], zero[:]), d_z, t)
        DVE.put(lambda e: e.tensor_copy(SUb[:], C[:, C_SU:C_SU + 128]), T["ld"])
        T["consts"] = T["mac", 0] = DVE.put(lambda e: e.tensor_copy(stepb[:], C[:, C_STEP:C_STEP + 1].broadcast_to((128, 128))), T["ld"])

        def weave(*gens):
            gens = list(gens)
            while gens:
                for g in list(gens):
                    if next(g, gens) is gens:
                        gens.remove(g)

        POOL.run(lambda e: None, T["mh"])
        weave(ln(0))
        norm_q(0)
        DVE.run(lambda e: None, T["ld2"], T["tg"])
        PE.run(lambda e: None, T["ld"], T["ld2"])
        POOL.run(lambda e: None, T["ld2"])
        on = lambda f, b: [f(b)] if 0 <= b < B else []
        for s_ in range(B + 3):
            if s_ < B:
                qk(s_, (0, 1))
            if 0 <= s_ - 2 < B:
                norm_t(s_ - 2)
            if s_ < B:
                qk(s_, (2, 3))
            if 2 <= s_ + 2 < B:
                load_k(s_ + 2)
            if s_ >= 3:
                before(s_ - 3)
                weave(rank(s_ - 3))
                weave(one_hots(s_ - 3))
            if s_ + 1 < B:
                weave(ln(s_ + 1))
                norm_q(s_ + 1)
            if 0 <= s_ - 1 < B:
                av(s_ - 1)
                add_x(s_ - 1)
            if s_ >= 3:
                table(s_ - 3)
            if 0 <= s_ - 2 < B:
                logits(s_ - 2)
            if 1 <= s_ and s_ + 2 < B:
                load_x(s_ + 2)
            if 1 <= s_ and s_ + 1 < B:
                load_v(s_ + 1)
            if s_ == 3:
                load_w(0)
                landed(0)
            weave(*on(ffn_in, s_ - 1), *on(choose, s_ - 2))

        for c in range(NCH):
            w = slice(c * CW, c * CW + CW)
            t = ACT.put(lambda e, w=w: e.copy(Wh[:, 0, w], Wf[:, 0, w]), (s_raw[0], 1), on=s_hi)
            T["lo0"] = POOL.put(lambda e, w=w: e.tensor_tensor(Wl[:, 0, w], Wf[:, 0, w], Wh[:, 0, w].bitcast(F32), ALU.subtract), t, on=s_lo)

        t = PE.put(lambda e: e.matmul(ps[6][:, 64:64 + E], ones[:], Mac[:, B, :], start=True, stop=True), T["mac", B])
        t = DVE.put(lambda e: e.tensor_scalar(Ni[:], ps[6][:, 64:64 + E], 127.0, None, op0=ALU.add), t)
        t = DVE.put(lambda e: e.tensor_scalar(Ti[:], Ni[:], 7, None, op0=ALU.arith_shift_right), t)
        t = DVE.put(lambda e: e.tensor_scalar(Tf[:], Ti[:], 1.0, None, op0=ALU.max), t)
        tf = t
        t = DVE.put(lambda e: e.tensor_tensor_scan(Ee[:], Tf[:], Tf[:], 0.0, ALU.add, ALU.bypass), t)
        te_ = t
        t = DVE.put(lambda e: e.tensor_tensor(Tx[:, 0:E], Ee[:], Tf[:], ALU.subtract), t)
        t = DVE.put(lambda e: e.tensor_tensor(us[:], C[:, C_SEL:C_SEL + 51].rearrange("p (c e) -> p c e", c=3),
                                             Tx[:].unsqueeze(1).broadcast_to((128, 3, E + 1)), ALU.mult), t)
        t = DVE.put(lambda e: e.tensor_reduce(uu[:], us[:], AX, ALU.add), t)
        for c in range(2):
            ts = DVE.put(lambda e, c=c: e.tensor_scalar(Sm[:, c, :], iota(NTP), uu[:, c:c + 1], None, op0=ALU.is_equal), t)
        tc = DVE.put(lambda e: e.tensor_scalar(cm[:], iota(NTP), uu[:, 2:3], None, op0=ALU.is_ge), t)

        p = ACT.put(lambda e: e.copy(tab[:], ps[7][:, 0:VT]), T["tb", B - 1])

        def mm(e):
            for c in range(2):
                m = e.transpose(ps[4][:, 128 * c:128 * c + 128], tab[:, 128 * c:128 * c + 128], idm)
            return m

        p = PE.put(mm, p, T["tTc", 0])
        p = ACT.put(lambda e: e.copy(tabT[:], ps[4][:, 0:256].rearrange("p (c t) -> p c t", c=2)), p)

        def mm(e):
            for c in range(2):
                m = e.matmul(ps[6][:, 0:NTP], tabT[:, c, :], Sm[:, c, :], start=(c == 0), stop=(c == 1))
            return m

        p = PE.put(mm, p, ts, tf, T[("prr",)], T[("lgr",)])
        T["src"] = DVE.put(lambda e: e.tensor_scalar(src[:], ps[6][:, 0:NTP], -1.0, 0.0, op0=ALU.add, op1=ALU.max), p)
        t = DVE.put(lambda e: e.tensor_scalar(iv[:], ps[6][:, 0:NTP], 0.0, C[:, C_PAD:C_PAD + 1], op0=ALU.is_equal, op1=ALU.mult), p)
        T["dst"] = DVE.put(lambda e: e.scalar_tensor_tensor(dst[:], ps[6][:, 0:NTP], -1.0, iv[:], ALU.add, ALU.add), t)

        def mm(e):
            e.matmul(ps[5][:, 0:NTP], ones[:], cm[:], start=True, stop=True)
            return e.matmul(ps[5][:, NTP:2 * NTP], stepb[:], cm[:], start=True, stop=True)

        p = PE.put(mm, tc, T["tTc", 1])
        DVE.put(lambda e: e.tensor_copy(te[:, 0:2, :], ps[5][:, 0:2 * NTP].rearrange("p (a t) -> p a t", a=2)), p)
        T["tabs"] = DVE.put(lambda e: e.tensor_scalar(te[:, 2, :], ps[5][:, 0:NTP], 4.0, 4.0, op0=ALU.mult, op1=ALU.add), p)
        T["ends"] = DVE.put(lambda e: e.tensor_copy(Ei[:], Ee[:]), te_)
        t = DVE.put(lambda e: e.tensor_tensor(ut[:], C[:, C_CNT:C_CNT + 32].rearrange("p (c e) -> p c e", c=2),
                                             Tf[:].unsqueeze(1).broadcast_to((128, 2, E)), ALU.mult), tf)
        t = DVE.put(lambda e: e.tensor_reduce(un[:], ut[:], AX, ALU.add), t)
        t = DVE.put(lambda e: e.tensor_copy(cntb[:], un[:].unsqueeze(2).broadcast_to((128, 2, 128))), t)

        def mm(e):
            e.matmul(ps[5][:, 160:160 + NTP], cntb[:, 0, :], cm[:], start=True, stop=True)
            return e.matmul(ps[5][:, 240:240 + NTP], cntb[:, 1, :], cm[:], start=True, stop=True)

        p = PE.put(mm, t)
        t = DVE.put(lambda e: e.tensor_tensor(j4[:], iota(NTP), ps[5][:, 160:160 + NTP], ALU.subtract), p)
        tn_ = DVE.put(lambda e: e.tensor_scalar(Tm[:], Tf[:, 0:1], -1.0, None, op0=ALU.add))
        tn_ = DVE.put(lambda e: e.tensor_scalar(iv[:], ps[5][:, 240:240 + NTP], Tm[:, 0:1], 1.0, op0=ALU.add, op1=ALU.max), p, T["dst"], tn_)
        t = DVE.put(lambda e: e.tensor_scalar(j4[:], j4[:], 4.0, None, op0=ALU.mult), t)
        for m_ in range(NCH):
            t = DVE.put(lambda e, m_=m_: e.scalar_tensor_tensor(fl[m_][:], iv[:], float(m_ + 1), j4[:], ALU.mult, ALU.is_le), t, tn_)
        for m_ in range(1, NCH):
            t = DVE.put(lambda e, m_=m_: e.tensor_tensor(fl[0][:], fl[0][:], fl[m_][:], ALU.add), t)
        t = DVE.put(lambda e: e.tensor_tensor(fl[0][:], fl[0][:], te[:, 2, :], ALU.add), t, T["tabs"])
        T["cp"] = DVE.put(lambda e: e.tensor_scalar(te[:, 3, :], fl[0][:], float(NCH * E), None, op0=ALU.min), t)

        load_w(1, T["av", B - 1])
        load_w(2, T["av", B - 1], T["tb", B - 1])
        def refill(e_):
            def w(e):
                v = e.value_load(Ei[0:1, e_ - 3:e_ - 2], min_val=1, max_val=NT)
                e.wait_ge(s_yb[0], v)
            SP.run(w, T["ends"])
            load_w(e_)

        landed(1)
        landed(2)
        for e_ in range(3, E):
            refill(e_)
            landed(e_)

        def gather(t):
            w = was("tx", t - 4) + was("gc", t - 4) + ([T["src"], T["st_row", B - 1], T["st_row", B - 2]] if t < 4 else [])
            T["ga", t] = POOL.dma(lambda e: e.indirect_dma_start(
                xg[t % 4][:], None, rows, bass.IndirectOffsetOnAxis(src[:, t:t + 1], axis=0)), d_g[t % 4], *w)

        def scatter(t):
            w = was("sca", t - 1) if t else [T["dst"], T["st_base", B - 1], T["st_base", B - 2], T["zero"]]
            T["sca", t] = POOL.dma(lambda e: e.indirect_dma_start(
                out, bass.IndirectOffsetOnAxis(dst[:, t:t + 1], axis=0), ys[t % 3][:], None, compute_op=ALU.add), d_s, T["ys", t], *w)

        R = {}

        def slot(e, t, load=False):
            if load:
                R[e, t] = e.value_load(te[0:1, 1, t:t + 1], min_val=0, max_val=2)
            return R[e, t]

        PX, PA, PB_, PT, PY = ps[0], ps[1], ps[2], ps[3], ps[4]
        PASSES = ((0, 0), (1, 0), (0, 1))

        def chunks(e, t):
            g0 = e.value_load(te[0:1, 3, t:t + 1], min_val=NCH, max_val=NCH * E)
            g1 = e.value_load(te[0:1, 3, t + 1:t + 2], min_val=NCH, max_val=NCH * E)
            return g0, g1

        def place(g):
            return slice(None), bass.ds((g >> 2) % 3, 1), bass.ds((g % NCH) * CW, CW)

        ACT.run(lambda e: None, T["st_base", B - 1], T["st_row", B - 1], T["st_base", B - 2], T["st_row", B - 2], T["zero"])

        def make_hi(t):
            def f(e):
                g0, g1 = chunks(e, t)
                with e.If(g0 < g1):
                    with e.Fori(g0, g1) as g:
                        e.wait_ge(s_raw[0], e.snap((g >> 2) + 1))
                        w = place(g)
                        e.copy(Wh[w], Wf[w]).then_inc(s_hi[0], 1)
            ACT.run(f, T["cp"])

        def make_lo(t):
            def f(e):
                g0, g1 = chunks(e, t)
                with e.If(g0 < g1):
                    with e.Fori(g0, g1) as g:
                        e.wait_ge(s_hi[0], e.snap(g + 1))
                        w = place(g)
                        e.tensor_tensor(Wl[w], Wf[w], Wh[w].bitcast(F32), ALU.subtract).then_inc(s_lo[0], 1)
            POOL.run(f, T["cp"])

        def trans_x(t):
            i = t % 2

            def tr(e):
                for c in range(4):
                    m = e.transpose(PX[:, 128 * c:128 * c + 128], xg[t % 4][:, 128 * c:128 * c + 128], idm)
                return m
            T["tx", t] = PE.put(tr, T["ga", t], *(was("xTl", t - 1) if t else [T["sc", B - 1]]))
            px = PX[:].rearrange("p (c t) -> p c t", c=4)
            k = ACT.put(lambda e: e.copy(xTh[i][:], px), T["tx", t], *was("l1b", t - 2))
            T["xTl", t] = DVE.put(lambda e: e.tensor_tensor(xTl[i][:], px, xTh[i][:].bitcast(F32), ALU.subtract), k)

        def gate(t):
            def gc(e):
                r = e.value_load(te[0:1, 0, t:t + 1], min_val=0, max_val=E - 1)
                return e.copy(gcol[t % 4][:], xg[t % 4][:, H:ROW][:, bass.ds(r, 1)])
            T["gc", t] = ACT.put(gc, T["ga", t], T["tabs"], *was("ys", t - 4))

        def product(e, P_, lh, r, col):
            n = 0
            for c in range(4):
                for xl, wl in PASSES:
                    at_ = CW * c + col
                    m = e.matmul(P_[:], lh[xl][:, c, :], (Wh, Wl)[wl][:, bass.ds(r, 1), at_:at_ + H], start=(n == 0), stop=(n == 11))
                    n += 1
            return m

        def l1(t, half):
            P_ = (PA, PB_)[half]

            def mm(e):
                if half == 0:
                    made = e.value_load(te[0:1, 2, t:t + 1], min_val=NCH, max_val=NCH * E)
                    slot(e, t, True)
                    e.wait_ge(s_lo[0], made)
                return product(e, P_, (xTh[t % 2], xTl[t % 2]), slot(e, t), H * half)
            T["l1" + "ab"[half], t] = PE.put(mm, T["xTl", t], T["tabs"], *was("h" + "ab"[half], t - 1))

        def act_a(t):
            def f(e):
                r = slot(e, t, True)
                return e.tensor_tensor(av_[:], PA[:], Bs[:, bass.ds(r, 1), 0:H], ALU.add)
            k = T["ha", t] = DVE.put(f, T["l1a", t], T["tabs"], *was("h", t - 1), *was("sg", t - 1))
            k = DVE.put(lambda e: e.tensor_scalar(av_[:], av_[:], LIMIT, None, op0=ALU.min), k)
            T["a", t] = k

        def sigm(t):
            T["sg", t] = ACT.put(lambda e: e.activation(sg[:], av_[:], AF.Sigmoid, scale=ALPHA), T["a", t], *was("h", t - 1))

        def act_b(t):
            k = T["hb", t] = DVE.put(lambda e: e.tensor_tensor(bv_[:], PB_[:], Bs[:, bass.ds(slot(e, t), 1), H:2 * H], ALU.add),
                                     T["l1b", t])
            k = DVE.put(lambda e: e.tensor_scalar(bv_[:], bv_[:], LIMIT, -LIMIT, op0=ALU.min, op1=ALU.max), k)
            k = DVE.put(lambda e: e.scalar_tensor_tensor(bv_[:], bv_[:], 1.0, av_[:], ALU.add, ALU.mult), k)
            T["h", t] = DVE.put(lambda e: e.tensor_tensor(hh[:], bv_[:], sg[:], ALU.mult), k, T["sg", t], *was("ta", t - 1))

        def trans_a(t):
            def tr(e):
                for c in range(4):
                    m = e.transpose(PT[:, 128 * c:128 * c + 128], hh[:, 128 * c:128 * c + 128], idm)
                return m
            T["ta", t] = PE.put(tr, T["h", t], *was("aTl", t - 1))
            pt = PT[:].rearrange("p (c t) -> p c t", c=4)
            k = ACT.put(lambda e: e.copy(aTh[:], pt), T["ta", t], *was("l2", t - 1))
            T["aTl", t] = DVE.put(lambda e: e.tensor_tensor(aTl[:], pt, aTh[:].bitcast(F32), ALU.subtract), k)

        def l2(t):
            T["l2", t] = PE.put(lambda e: product(e, PY, (aTh, aTl), slot(e, t, t + 1 in ENDS), 2 * H), T["aTl", t], *was("yb", t - 1))

        def out_y(t):
            y = ys[t % 3]
            T["yb", t] = DVE.put(lambda e: e.tensor_tensor(y[:], PY[:], Bs[:, bass.ds(slot(e, t, t + 1 in ENDS), 1), 2 * H:CW], ALU.add),
                                 T["l2", t], *was("sca", t - 3), on=s_yb)
            T["ys", t] = ACT.put(lambda e: e.activation(y[:], y[:], AF.Copy, scale=gcol[t % 4][:]), T["yb", t], T["gc", t])

        gather(0)
        gather(1)
        gather(2)
        trans_x(0)
        gate(0)
        def start(t):
            l1(t, 0)
            act_a(t)
            if t >= 1:
                trans_a(t - 1)
            if t + 3 < NT:
                gather(t + 3)
            if t + 1 < NT:
                trans_x(t + 1)
                gate(t + 1)
            sigm(t)
            make_hi(t)
            make_lo(t)
            l1(t, 1)
            act_b(t)
            if t >= 1:
                l2(t - 1)
                out_y(t - 1)
                scatter(t - 1)

        def finish(t):
            trans_a(t - 1)
            l2(t - 1)
            out_y(t - 1)
            scatter(t - 1)
            POOL.run(lambda e: None, T["sca", t - 1], *[T["ga", u] for u in range(t, min(t + 3, NT))])

        tiles = (PE, ACT, DVE, POOL)

        def only(t, more):
            def cond(e):
                n = e.value_load(Ei[0:1, E - 1:E], min_val=1, max_val=NT)
                return n > t if more else n <= t
            for line in tiles:
                line.only(cond)

        def close(n=1):
            for line in tiles * n:
                line.close()

        for t in range(NT):
            if t in ENDS:
                kept = [(line.n, dict(line.seen)) for line in tiles], [c[1] for c in chans], dict(T)
                only(t, False)
                finish(t)
                close()
                for line, (n, seen) in zip(tiles, kept[0]):
                    line.n, line.seen = n, seen
                for c, n in zip(chans, kept[1]):
                    c[1] = n
                T.clear()
                T.update(kept[2])
                if t != ENDS[0]:
                    close()
                only(t, True)
            start(t)
        finish(NT)
        close()

        block = es.enter_context(nc.Block())

        @block.sync
        def _(e):
            SP.emit(e)

        @block.scalar
        def _(e):
            ACT.emit(e)

        @block.gpsimd
        def _(e):
            POOL.emit(e)

        @block.vector
        def _(e):
            DVE.emit(e)

        @block.tensor
        def _(e):
            PE.emit(e)


def lay_out(x, ctx_2048, g_xattn, g_ffn, L0_ffn_norm_w, L0_ffn_gate_w, L0_ffn_gate_b, L0_ffn_w1, L0_ffn_b1, L0_ffn_w2, L0_ffn_b2):
    f = lambda a: np.asarray(a)
    w1 = f(L0_ffn_w1).reshape(E, H, 2, 4, 128)
    w2 = f(L0_ffn_w2).reshape(E, H, 4, 128)
    wts = np.empty((E, 128, 4, 3, H), np.float32)
    wts[:, :, :, 0:2] = w1.transpose(0, 4, 3, 2, 1)
    wts[:, :, :, 2] = w2.transpose(0, 3, 2, 1)
    b1 = f(L0_ffn_b1).reshape(E, H, 2)
    bias = np.concatenate([b1[:, :, 0], b1[:, :, 1], f(L0_ffn_b2)], axis=1)
    ctxT = f(ctx_2048).transpose(0, 2, 1).reshape(B, 4, 128, S).transpose(0, 2, 1, 3)
    gw = f(L0_ffn_gate_w).reshape(E, 4, 128).transpose(2, 1, 0)
    return dict(x=f(x).reshape(M, H), ctx=f(ctx_2048), ctxT=ctxT, gx=f(g_xattn), gf=f(g_ffn), nw=f(L0_ffn_norm_w), gw=gw,
                gb=f(L0_ffn_gate_b), wts=wts.reshape(E, 128, WS), bias=bias, cst=shape_constants())


def kernel(**inputs):
    import concourse.bacc as _bacc
    from concourse.bass_utils import run_bass_kernel_spmd as _run

    nc = _bacc.Bacc("TRN2", target_bir_lowering=False, num_devices=1)
    arrays, args = {}, {}
    for name, a in lay_out(**inputs).items():
        a = np.ascontiguousarray(a)
        arrays[f"in_{name}"] = a
        args[name] = nc.dram_tensor(f"in_{name}", a.shape, mybir.dt.from_np(a.dtype), kind="ExternalInput").ap()
    args["out"] = nc.dram_tensor("out_0", (M + 128, H), F32, kind="ExternalOutput").ap()
    build(nc, **args)
    r = _run(nc, [arrays], core_ids=[0])
    return r.results[0]["out_0"][:M].reshape(B, S, H)
```

```python
from contextlib import ExitStack

import numpy as np

import concourse.bass as bass
from concourse import mybir

ALU = mybir.AluOpType
AF = mybir.ActivationFunctionType
F32 = mybir.dt.float32
F32R = mybir.dt.float32r
BF16 = mybir.dt.bfloat16
F16 = mybir.dt.float16
I32 = mybir.dt.int32
U32 = mybir.dt.uint32
AX = mybir.AxisListType.X

B = 8
S = 256
H = 512
E = 16
K = 4
M = B * S
NI = M // 128
NT = M * K // 128 + E - 1
ENDS = (72, 75)
VT = E * NI
NTP = 80
ROW = H + E
WS = 4 * 1536
NCH = 4
CW = 1536
SPLIT = 3
POOL_HOTS = (3, 7)
EPS = 1e-5
LIMIT = 7.0
ALPHA = 1.702

C_ID = 0
C_SU = 128
C_IOTA = 256
C_TOK = 512
C_SEL = 528
C_CNT = 579
C_STEP = 611
C_PAD = 612
C_N = 613


def shape_constants():
    c = np.zeros((128, C_N), np.float32)
    p = np.arange(128)
    c[:, C_ID:C_ID + 128] = np.eye(128)
    c[:, C_SU:C_SU + 128] = p[:, None] < p[None, :]
    c[:, C_IOTA:C_IOTA + 256] = np.arange(256)
    c[:, C_TOK:C_TOK + NI] = 128 * np.arange(NI) + p[:, None] + 1
    sel = np.zeros((128, 3, E + 1), np.float32)
    for h in range(2):
        sel[p, h, 8 * h + p // 16] = 1
        sel[:, h, E] = p % 16
    for q in range(128):
        if q < E - 1:
            sel[q, 2, q + 1] = 1
        else:
            sel[q, 2, E] = 1000
    c[:, C_SEL:C_SEL + 51] = sel.reshape(128, 51)
    q = p[:E - 1]
    cnt = np.zeros((128, 2, E), np.float32)
    cnt[q, 0, q] = 1
    cnt[q, 1, q + 1] = 1
    cnt[q, 1, q] = -1
    c[:, C_CNT:C_CNT + 32] = cnt.reshape(128, 32)
    c[:E - 1, C_STEP] = (q + 1) % 3 - q % 3
    c[:, C_PAD] = M + 1 + p
    return c


class Line:

    def __init__(self, name, sem):
        self.name, self.sem, self.n, self.items, self.seen = name, sem, 0, [], {}

    def put(self, fn, *waits, on=None):
        if on is not None:
            on[1] += 1
            self._push(fn, waits, (on[0], 1))
            return (on[0], on[1])
        self.n += 1
        self._push(fn, waits, (self.sem, 1))
        return (self.sem, self.n)

    def dma(self, fn, chan, *waits):
        chan[1] += 16
        self._push(fn, waits, (chan[0], 16))
        return (chan[0], chan[1])

    def only(self, cond):
        self.items.append((cond, None, "if"))

    def close(self):
        self.items.append((None, None, "end"))

    def run(self, fn, *waits):
        self._push(fn, waits, None)

    def _push(self, fn, waits, inc):
        need = []
        for sem, val in waits:
            if self.seen.get(sem.name, 0) < val:
                self.seen[sem.name] = val
                need.append((sem, val))
        self.items.append((fn, need, inc))

    def emit(self, eng):
        inside = []
        for fn, need, inc in self.items:
            if inc == "if":
                inside.append(ExitStack())
                inside[-1].enter_context(eng.If(fn(eng)))
            elif inc == "end":
                inside.pop().close()
            else:
                for sem, val in need:
                    eng.wait_ge(sem, val)
                ins = fn(eng)
                if inc is not None:
                    ins.then_inc(*inc)


def build(nc, x, ctx, ctxT, gx, gf, nw, gw, gb, wts, bias, cst, out):
    with ExitStack() as es:
        rows = nc.dram_tensor("rows", (M, ROW), F32, kind="Internal").ap()

        top = [16512]

        def at(name, shape, dt, offset):
            return nc.alloc_sbuf_tensor_at(name, shape, dt, offset=offset)

        def sb(name, shape, dt=F32):
            n = int(np.prod(shape[1:])) * mybir.dt.size(dt)
            t = at(name, shape, dt, top[0])
            top[0] += (n + 31) // 32 * 32
            return t

        HI = top[0]
        RAW = HI + 12 * WS
        BIAS = RAW + 12 * WS
        REST = BIAS + 12 * CW
        Wh = at("Wh", [128, 3, WS], F32R, HI)
        Wf = at("Wf", [128, 3, WS], F32, RAW)
        Wl = at("Wl", [128, 3, WS], F32R, RAW)
        Bs = at("Bs", [128, 3, CW], F32, BIAS)

        top[0] = REST
        C = sb("C", [128, C_N])
        te = sb("te", [128, 5, NTP], I32)
        src = sb("src", [128, NTP], I32)
        dst = sb("dst", [128, NTP], I32)
        Ei = sb("Ei", [128, E], I32)
        gcol = [sb(f"gcol{i}", [128, 1]) for i in range(4)]
        ones = sb("ones", [128, 128], BF16)
        stepb = sb("stepb", [128, 128], BF16)
        cntb = sb("cntb", [128, 2, 128], BF16)
        Ni = sb("Ni", [128, E], I32)
        Ti = sb("Ti", [128, E], I32)
        Tf = sb("Tf", [128, E])
        Ee = sb("Ee", [128, E])
        Tx = sb("Tx", [128, E + 1])
        us = sb("us", [128, 3, E + 1])
        uu = sb("uu", [128, 3])
        ut = sb("ut", [128, 2, E])
        un = sb("un", [128, 2])
        Sm = sb("Sm", [128, 2, NTP])
        cm = sb("cm", [128, NTP], BF16)
        tab = sb("tab", [128, VT])
        tabT = sb("tabT", [128, 2, 128])
        iv = sb("iv", [128, NTP])
        j4 = sb("j4", [128, NTP])
        fl = [sb(f"fl{i}", [128, NTP]) for i in range(NCH)]
        Tm = sb("Tm", [128, 1])
        tail = top[0]

        xg = [sb(f"xg{i}", [128, ROW]) for i in range(4)]
        xTh = [sb(f"xTh{i}", [128, 4, 128], F32R) for i in range(2)]
        xTl = [sb(f"xTl{i}", [128, 4, 128], F32R) for i in range(2)]
        av_ = sb("av_", [128, H])
        sg = sb("sg", [128, H])
        bv_ = sb("bv_", [128, H])
        hh = sb("hh", [128, H])
        aTh = sb("aTh", [128, 4, 128], F32R)
        aTl = sb("aTl", [128, 4, 128], F32R)
        ys = [sb(f"ys{i}", [128, H]) for i in range(3)]
        small = top[0]

        def pair(name, shape, n):
            o = top[0]
            f = [sb(f"{name}{i}", shape) for i in range(n)]
            end, top[0] = top[0], o
            l = [sb(f"{name}l{i}", shape, F32R) for i in range(n)]
            assert top[0] == end
            return f, l

        top[0] = RAW + 4 * WS
        (Sc,), (Sl,) = pair("Sc", [128, 4, H], 1)
        Sh = sb("Sh", [128, 4, H], F32R)
        (Qt,), (Ql,) = pair("Qt", [128, 2, H], 1)
        Qh = sb("Qh", [128, 2, H], F32R)
        assert top[0] <= RAW + 8 * WS
        Kt, Kl = pair("Kt", [128, 2, H], 2)
        Vt, Vl = pair("Vt", [128, 4, S], 2)
        Kh = [sb(f"Kh{i}", [128, 2, H], F32R) for i in range(2)]
        assert top[0] <= BIAS
        top[0] = BIAS + 8 * CW
        OV = sb("OV", [128, 2 * K, VT], F16)
        OL = sb("OL", [128, 2 * K, 128], F16)
        assert top[0] <= REST
        top[0] = HI + 4 * WS
        X = [sb(f"X{i}", [128, 2, H]) for i in range(3)]
        x1 = [sb(f"x1_{i}", [128, 2, H]) for i in range(2)]
        tt = [sb(f"tt{i}", [128, 2, ROW]) for i in range(2)]
        base = [sb(f"base{i}", [128, 2, H]) for i in range(2)]
        tTs = [sb(f"tTs{i}", [128, 4, 128]) for i in range(2)]
        nwb = sb("nwb", [128, H])
        zero = sb("zero", [128, H])
        assert top[0] <= RAW

        top[0] = tail
        gwT = sb("gwT", [128, 4, E])
        gbb = sb("gbb", [128, E])
        gg = sb("gg", [128, 2])
        tg = sb("tg", [128, 2])
        tn = sb("tn", [128, 2])
        mh = sb("mh", [128, 4])
        SUb = sb("SUb", [128, 128], BF16)
        io16 = sb("io16", [128, VT], F16)
        Mac = sb("Mac", [128, B + 1, E], BF16)
        st = sb("st", [128, 2, 6])
        mv = [sb(f"mv{i}", [128, 2, 2]) for i in range(2)]
        ve = [sb(f"ve{i}", [128, 2]) for i in range(2)]
        rs = [sb(f"rs{i}", [128, 2]) for i in range(2)]
        nb = [sb(f"nb{i}", [128, 2]) for i in range(2)]
        st1 = sb("st1", [128, 2, 6])
        mv1 = [sb(f"mv1_{i}", [128, 2, 2]) for i in range(2)]
        ve1 = [sb(f"ve1_{i}", [128, 2, 2]) for i in range(2)]
        rs1 = [sb(f"rs1_{i}", [128, 2, 2]) for i in range(2)]
        c1 = [sb(f"c1_{i}", [128, 2]) for i in range(2)]
        mc = [sb(f"mc_{i}", [128, 2]) for i in range(2)]
        nt = [sb(f"nt_{i}", [128, 2]) for i in range(2)]
        Lg = sb("Lg", [128, 2, E])
        mx = sb("mx", [128, 2, 8])
        ix = sb("ix", [128, 2, 8], U32)
        dd = sb("dd", [128, 2, K])
        s1 = sb("s1", [128, 2, K])
        s2 = sb("s2", [128, 2, K])
        ex = sb("ex", [128, 2, K])
        zz = sb("zz", [128, 2])
        gk = sb("gk", [128, 2, K])
        idf = [sb(f"idf{i}", [128, 2, K]) for i in range(2)]
        oh = [sb(f"oh{i}", [128, 2, K, E]) for i in range(2)]
        og = sb("og", [128, 2, K, E])
        op = sb("op", [128, 2, K, E])
        mk = [sb(f"mk{i}", [128, 2, E], BF16) for i in range(2)]
        ms = sb("ms", [128, E], BF16)
        rr = sb("rr", [128, 2 * K])
        rh = sb("rh", [128, 2 * K], I32)
        vt = sb("vt", [128, 2 * K])
        lof = sb("lof", [128, 2 * K])
        Vh = [sb(f"Vh{i}", [128, 4, S], F32R) for i in range(2)]
        assert max(top[0], small) <= 229368, (top[0], small)

        ps = [es.enter_context(nc.psum_tensor(f"ps{i}", [128, 512], F32)) for i in range(8)]

        sem = lambda n: es.enter_context(nc.semaphore(n))
        chans = []

        def chan(n):
            chans.append([sem(n), 0])
            return chans[-1]

        s_raw = chan("s_raw")
        s_hi = chan("s_hi")
        s_lo = chan("s_lo")
        s_yb = chan("s_yb")
        PE, ACT, DVE, POOL, SP = [Line(n, sem(n)) for n in ("pe", "act", "dve", "pool", "sp")]
        d_c = chan("d_c")
        d_c2 = chan("d_c2")
        d_gg = chan("d_gg")
        d_x = [chan(f"d_x{i}") for i in range(3)]
        d_k = [chan(f"d_k{i}") for i in range(2)]
        d_v = [chan(f"d_v{i}") for i in range(2)]
        d_o = [chan(f"d_o{i}") for i in range(2)]
        d_r = [chan(f"d_r{i}") for i in range(2)]
        d_z = chan("d_z")
        d_w = [chan(f"d_w{i}") for i in range(3)]
        d_f = [chan(f"d_f{i}") for i in range(NCH)]
        d_b = chan("d_b")
        d_g = [chan(f"d_g{i}") for i in range(4)]
        d_s = chan("d_s")

        xb = x.rearrange("(b j p) h -> b p j h", j=2, p=128)
        cb = ctx.rearrange("b (j p) h -> b p j h", p=128)
        ob = out[0:M, :].rearrange("(b j p) h -> b p j h", j=2, p=128)
        rb = rows.rearrange("(b j p) h -> b p j h", j=2, p=128)

        idm = C[:, C_ID:C_ID + 128]
        iota = lambda n: C[:, C_IOTA:C_IOTA + n]
        T = {}
        was = lambda *key: [T[key]] if key in T else []

        def load_x(b):
            T["lx", b] = SP.dma(lambda e: e.dma_start(X[b % 3][:], xb[b]), d_x[b % 3], *was("x1", b - 3, 1))

        def load_k(b):
            T["lk", b] = SP.dma(lambda e: e.dma_start(Kt[b % 2][:], cb[b]), d_k[b % 2], *was("qk", b - 2))

        def load_v(b):
            T["lv", b] = SP.dma(lambda e: e.dma_start(Vt[b % 2][:], ctxT[b]), d_v[b % 2], *was("av", b - 2))

        def ln(b):
            i = b % 2
            for j in range(2):
                t = DVE.put(lambda e, j=j: e.bn_stats(st[:, j, :], X[b % 3][:, j, :]), T["lx", b])
                yield
            for j in range(2):
                t = DVE.put(lambda e, j=j: e.bn_aggr(mv[i][:, j, :], st[:, j, :]), t, *was("nq", b - 2))
                yield
            t = DVE.put(lambda e: e.tensor_scalar(ve[i][:], mv[i][:, :, 1], EPS, None, op0=ALU.add), t)
            T["rs", b] = POOL.put(lambda e: e.tensor_tensor(rs[i][:], ve[i][:], mh[:, 0:2], ALU.pow), t)
            yield

        def ln_bias(b):
            i = b % 2
            T["nb", b] = DVE.put(lambda e: e.scalar_tensor_tensor(nb[i][:], mv[i][:, :, 0], -1.0, rs[i][:], ALU.mult, ALU.mult), T["rs", b])
            yield

        def norm_q(b):
            for dst_, key in ((Qt, "qf"), (Qh, "qh")):
                for j in range(2):
                    T[key, j] = T["nq", b] = ACT.put(lambda e, j=j, dst_=dst_: e.activation(
                        dst_[:, j, :], X[b % 3][:, j, :], AF.Identity, bias=nb[b % 2][:, j:j + 1], scale=rs[b % 2][:, j:j + 1]),
                        T["nb", b], *was("qk", b - 1))

        def low_q(b, j):
            T["ql", b, j] = DVE.put(lambda e: e.tensor_tensor(Ql[:, j, :], Qt[:, j, :], Qh[:, j, :].bitcast(F32), ALU.subtract),
                                    T["qf", j], T["qh", j])

        def split_k(b):
            i = b % 2
            t = ACT.put(lambda e: e.copy(Kh[i][:], Kt[i][:]), T["lk", b], *was("qk", b - 2))
            T["kl", b] = POOL.put(lambda e: e.tensor_tensor(Kl[i][:], Kt[i][:], Kh[i][:].bitcast(F32), ALU.subtract), t)

        def split_v(b, low):
            i = b % 2
            if not low:
                T["vh", b] = ACT.put(lambda e: e.copy(Vh[i][:, 0:SPLIT, :], Vt[i][:, 0:SPLIT, :]), T["lv", b], *was("av", b - 2))
            else:
                T["vl", b] = POOL.put(lambda e: e.tensor_tensor(Vl[i][:, 0:SPLIT, :], Vt[i][:, 0:SPLIT, :], Vh[i][:, 0:SPLIT, :].bitcast(F32), ALU.subtract), T["vh", b])

        PASSES = ((0, 0), (1, 0), (0, 1))

        def qk(b, c):
            def mm(e):
                n = 0
                for k in range(2):
                    for ql, kl in PASSES:
                        m = e.matmul(ps[c % 2][:], (Qh, Ql)[ql][:, k, 128 * c:128 * c + 128], (Kh, Kl)[kl][b % 2][:, k, :],
                                     start=(n == 0), stop=(n == 5))
                        n += 1
                return m
            T["qk", b] = T["qkc", c] = PE.put(mm, T["ql", b, 0], T["ql", b, 1], T["kl", b], *was("sg", c % 2))

        def score(b, c):
            for dst_ in (Sc, Sh)[:1 + (c < SPLIT)]:
                T["sg", c % 2] = ACT.put(lambda e, dst_=dst_: e.activation(dst_[:, c, :], ps[c % 2][:], AF.Sigmoid, scale=1.0 / 16.0),
                                         T["qkc", c], *was("av", b - 1))
            T["sh", c] = T["sc", b, c] = T["sg", c % 2]

        def low_s(b, c):
            T["sc", b, c] = DVE.put(lambda e: e.tensor_tensor(Sl[:, c, :], Sc[:, c, :], Sh[:, c, :].bitcast(F32), ALU.subtract), T["sh", c])

        def low_scores(b):
            for c in range(SPLIT):
                low_s(b, c)
                yield
                yield

        def av(b, j):
            i = b % 2
            for c in range(4):
                def mm(e, c=c):
                    if c >= SPLIT:
                        return e.matmul(ps[2 + j][:], Vt[i][:, c, 128 * j:128 * j + 128], Sc[:, c, :], start=(c == 0), stop=(c == 3))
                    for vl, sl in PASSES:
                        m = e.matmul(ps[2 + j][:], (Vh, Vl)[vl][i][:, c, 128 * j:128 * j + 128], (Sh, Sl)[sl][:, c, :],
                                     start=(c == 0 and vl + sl == 0), stop=(c == 3 and sl == 1))
                    return m
                T["av", b] = T["avj", j] = PE.put(mm, T["sc", b, c], T["vl", b], *was("x1j", j))

        def add_x(b, j):
            T["x1", b, j] = T["x1j", j] = DVE.put(
                lambda e: e.scalar_tensor_tensor(x1[b % 2][:, j, :], ps[2 + j][:], tg[:, 0:1], X[b % 3][:, j, :], ALU.mult, ALU.add),
                T["avj", j], T["tg"], *was("base", b - 2), *was("tn", b - 2))

        def ffn_in(b):
            i = b % 2
            for j in range(2):
                t = DVE.put(lambda e, j=j: e.bn_stats(st1[:, j, :], x1[b % 2][:, j, :]), T["x1", b, j])
                yield
            for j in range(2):
                t = DVE.put(lambda e, j=j: e.bn_aggr(mv1[i][:, j, :], st1[:, j, :]), t, *was("base", b - 2))
                yield
            t0 = DVE.put(lambda e: e.tensor_scalar(ve1[i][:, 0, :], mv1[i][:, :, 1], EPS, None, op0=ALU.add), t)
            yield
            t = DVE.put(lambda e: e.scalar_tensor_tensor(ve1[i][:, 1, :], ve1[i][:, 0, :], EPS, mv1[i][:, :, 1], ALU.mult, ALU.add), t0)
            T["rs1", b] = POOL.put(lambda e: e.tensor_tensor(rs1[i][:].rearrange("p a j -> p (a j)"), ve1[i][:].rearrange("p a j -> p (a j)"),
                                                             mh[:], ALU.pow), t)
            yield

        def ffn_bias(b):
            i, p = b % 2, T["rs1", b]
            T["nt", b] = DVE.put(lambda e: e.scalar_tensor_tensor(nt[i][:], mv1[i][:, :, 0], -1.0, rs1[i][:, 1, :], ALU.mult, ALU.mult), p)
            yield
            DVE.put(lambda e: e.tensor_scalar(c1[i][:], rs1[i][:, 0, :], tg[:, 1:2], 1.0, op0=ALU.mult, op1=ALU.add), p)
            yield
            T["mc", b] = DVE.put(lambda e: e.scalar_tensor_tensor(mc[i][:], rs1[i][:, 0, :], tn[:, 1:2], mv1[i][:, :, 0], ALU.mult, ALU.mult), p)
            yield

        def norm_t(b, j):
            i = b % 2
            T["tn", b] = ACT.put(lambda e: e.activation(tt[i][:, j, 0:H], x1[b % 2][:, j, :], AF.Identity, bias=nt[i][:, j:j + 1],
                                                        scale=rs1[i][:, 1, j:j + 1]), T["nt", b], *was("st_row", b - 2))
            T["t", b, j] = POOL.put(lambda e: e.tensor_tensor(tt[i][:, j, 0:H], tt[i][:, j, 0:H], nwb[:], ALU.mult), T["tn", b])

        def out_base(b):
            i = b % 2
            for j in range(2):
                T["base", b] = ACT.put(lambda e, j=j: e.activation(base[i][:, j, :], x1[b % 2][:, j, :], AF.Identity,
                                                                   bias=mc[i][:, j:j + 1], scale=c1[i][:, j:j + 1]),
                                        T["mc", b], *was("st_base", b - 2))

        def store_base(b):
            i = b % 2
            T["st_base", b] = SP.dma(lambda e: e.dma_start(ob[b], base[i][:]), d_o[i], T["base", b])

        def turn_t(b, j):
            def tr(e):
                for c in range(4):
                    m = e.transpose(ps[4 + j][:, 128 * c:128 * c + 128], tt[b % 2][:, j, 128 * c:128 * c + 128], idm)
                return m
            t = PE.put(tr, T["t", b, j], *was("tTc", j))
            T["tTc", j] = ACT.put(lambda e: e.copy(tTs[j][:], ps[4 + j][:].rearrange("p (c t) -> p c t", c=4)), t, *was("lgm", j))

        def logits(b):
            for j in range(2):
                def mm(e, j=j):
                    for c in range(4):
                        m = e.matmul(ps[6][:, 16 * j:16 * j + 16], tTs[j][:, c, :], gwT[:, c, :], start=(c == 0), stop=(c == 3))
                    return m
                T["lgm", j] = T["lg", b] = PE.put(mm, T["tTc", j], *was("lgr"), *was("prr"))

        def choose(b):
            i = b % 2
            t = T[("lgr",)] = DVE.put(lambda e: e.tensor_tensor(Lg[:], ps[6][:, 0:32].rearrange("p (j e) -> p j e", j=2),
                                                               gbb[:].unsqueeze(1).broadcast_to((128, 2, E)), ALU.add), T["lg", b])
            yield
            for j in range(2):
                t2 = DVE.put(lambda e, j=j: e.max(mx[:, j, :], Lg[:, j, :]), t)
                yield
            td = DVE.put(lambda e: e.tensor_tensor(dd[:], mx[:, :, 0:K], mx[:, :, 0:1].broadcast_to((128, 2, K)), ALU.subtract), t2)
            T["dd", b] = td
            yield
            for j in range(2):
                t2 = DVE.put(lambda e, j=j: e.max_index(ix[:, j, :], mx[:, j, :], Lg[:, j, :]), t2)
                yield
            t = DVE.put(lambda e: e.tensor_copy(idf[i][:], ix[:, :, 0:K]), t2)
            yield
            to = DVE.put(lambda e: e.tensor_tensor(
                oh[i][:].rearrange("p j k e -> p (j k) e"), idf[i][:].rearrange("p j k -> p (j k)").unsqueeze(2).broadcast_to((128, 2 * K, E)),
                iota(E).unsqueeze(1).broadcast_to((128, 2 * K, E)), ALU.is_equal), t)
            yield

            def red(e):
                with nc.allow_low_precision(reason="counts up to 4"):
                    return e.tensor_reduce(mk[i][:], oh[i][:].rearrange("p j k e -> p j e k"), AX, ALU.add)

            t = T["mk", b] = DVE.put(red, to, *was("pm", b - 2))
            p = POOL.put(lambda e: e.tensor_tensor(ms[:], mk[i][:, 0, :], mk[i][:, 1, :], ALU.add), t)
            T["mac", b + 1] = POOL.put(lambda e: e.tensor_tensor(Mac[:, b + 1, :], Mac[:, b, :], ms[:], ALU.add), p)
            yield

        def gate_sigmoids(b):
            ACT.put(lambda e: e.activation(s1[:], dd[:], AF.Sigmoid), T["dd", b])
            T["s2", b] = ACT.put(lambda e: e.activation(s2[:], dd[:], AF.Sigmoid, scale=-1.0))

        def gates(b):
            i, ts = b % 2, T["s2", b]
            t = DVE.put(lambda e: e.reciprocal(s2[:], s2[:]), ts)
            yield
            t = DVE.put(lambda e: e.tensor_tensor(ex[:], s1[:], s2[:], ALU.mult), t)
            yield
            t = DVE.put(lambda e: e.tensor_reduce(zz[:], ex[:], AX, ALU.add), t)
            yield
            t = DVE.put(lambda e: e.reciprocal(zz[:], zz[:]), t)
            yield
            t = DVE.put(lambda e: e.scalar_tensor_tensor(gk[:], ex[:], tg[:, 1:2], zz[:].unsqueeze(2).broadcast_to((128, 2, K)),
                                                         ALU.mult, ALU.mult), t)
            yield
            t = DVE.put(lambda e: e.tensor_tensor(
                og[:].rearrange("p j k e -> p (j k) e"), oh[i][:].rearrange("p j k e -> p (j k) e"),
                gk[:].rearrange("p j k -> p (j k)").unsqueeze(2).broadcast_to((128, 2 * K, E)), ALU.mult), t)
            yield
            t = DVE.put(lambda e: e.tensor_reduce(tt[i][:, :, H:ROW], og[:].rearrange("p j k e -> p j e k"), AX, ALU.add), t,
                        *was("st_row", b - 2))
            T["gates", b] = t
            yield

        def store_rows(b):
            i = b % 2
            T["st_row", b] = SP.dma(lambda e: e.dma_start(rb[b], tt[i][:]), d_r[i], T["gates", b], T["t", b, 0], T["t", b, 1])

        def before(b):
            i = b % 2

            def mm(e):
                e.matmul(ps[6][:, 32:48], SUb[:], mk[i][:, 0, :], start=True, stop=False)
                e.matmul(ps[6][:, 32:48], ones[:], Mac[:, b, :], start=False, stop=True)
                e.matmul(ps[6][:, 48:64], SUb[:], mk[i][:, 1, :], start=True, stop=False)
                e.matmul(ps[6][:, 48:64], ones[:], Mac[:, b, :], start=False, stop=False)
                return e.matmul(ps[6][:, 48:64], ones[:], mk[i][:, 0, :], start=False, stop=True)

            T["pm", b] = PE.put(mm, T["mk", b], T["mac", b], T["consts"], *was("prr"))

        def rank(b):
            i = b % 2
            t = T[("prr",)] = DVE.put(lambda e: e.tensor_tensor(
                op[:], oh[i][:], ps[6][:, 32:64].rearrange("p (j e) -> p j e", j=2).unsqueeze(2).broadcast_to((128, 2, K, E)), ALU.mult),
                T["pm", b])
            yield
            tr = DVE.put(lambda e: e.tensor_reduce(rr[:], op[:].rearrange("p j k e -> p (j k) e"), AX, ALU.add), t)
            yield
            th = DVE.put(lambda e: e.tensor_scalar(rh[:], rr[:], 1.0 / 128, -127.0 / 256, op0=ALU.mult, op1=ALU.add), tr)
            yield
            T["vt", b] = DVE.put(lambda e: e.scalar_tensor_tensor(vt[:], idf[i][:].rearrange("p j k -> p (j k)"), float(NI), rh[:],
                                                                  ALU.mult, ALU.add), th, *was("ov", b - 1, "pool"))
            yield
            T["lo", b] = DVE.put(lambda e: e.scalar_tensor_tensor(lof[:], rh[:], -128.0, rr[:], ALU.mult, ALU.add), th)
            yield

        def one_hot(b, q, eng):
            n = 2 * b + q // K
            T["ov", b, eng.name] = eng.put(lambda e: e.tensor_scalar(
                OV[:, q, :], io16[:], vt[:, q:q + 1], C[:, C_TOK + n:C_TOK + n + 1], op0=ALU.is_equal, op1=ALU.mult),
                T["vt", b], *was("tb", b - 1))

        def one_hots(b):
            for q in range(2 * K):
                T["ol", b] = DVE.put(lambda e, q=q: e.tensor_scalar(OL[:, q, :], io16[:, 0:128], lof[:, q:q + 1], None, op0=ALU.is_equal),
                                     T["lo", b], *was("tb", b - 1))
                yield
                if q not in POOL_HOTS:
                    one_hot(b, q, DVE)
                    yield

        def table(b):
            def mm(e):
                for q in range(2 * K):
                    m = e.matmul(ps[7][:, 0:VT], OL[:, q, :], OV[:, q, :], start=(b == 0 and q == 0), stop=(b == B - 1 and q == 2 * K - 1))
                return m
            T["tb", b] = PE.put(mm, T["ol", b], T["ov", b, "dve"], *was("ov", b, "pool"))

        def load_w(e_, *w):
            s_ = e_ % 3
            SP.dma(lambda e: e.dma_start(Wf[:, s_, :], wts[e_]), d_w[s_], *w)
            SP.dma(lambda e: e.dma_start(Bs[:, s_, :], bias[e_:e_ + 1, :].partition_broadcast(128)), d_w[s_])

        def load_first(c):
            T["lw0", c] = SP.dma(lambda e: e.dma_start(Wf[:, 0, c * CW:c * CW + CW], wts[0, :, c * CW:c * CW + CW]), d_f[c])
            if c == NCH - 1:
                SP.dma(lambda e: e.dma_start(Bs[:, 0, :], bias[0:1, :].partition_broadcast(128)), d_b)

        def landed(e_):
            if e_ == 0:
                SP.run(lambda e: e.wait_ge(d_b[0], 16))
            else:
                SP.run(lambda e: e.wait_ge(d_w[e_ % 3][0], 32 * ((e_ + 2) // 3)))
            SP.run(lambda e: e.sem_inc(s_raw[0], 1))

        load_x(0)
        SP.dma(lambda e: e.dma_start(gg[:, 0:1], gx.partition_broadcast(128)), d_gg)
        T["gg"] = SP.dma(lambda e: e.dma_start(gg[:, 1:2], gf.partition_broadcast(128)), d_gg)
        load_k(0)
        load_v(0)
        T["ld"] = SP.dma(lambda e: e.dma_start(C[:], cst), d_c)
        load_x(1)
        load_k(1)
        SP.dma(lambda e: e.dma_start(nwb[:], nw.partition_broadcast(128)), d_c2)
        SP.dma(lambda e: e.dma_start(gwT[:], gw), d_c2)
        T["ld2"] = SP.dma(lambda e: e.dma_start(gbb[:], gb.partition_broadcast(128)), d_c2)
        load_v(1)
        load_first(0)

        T["mh"] = POOL.put(lambda e: e.memset(mh[:], -0.5))
        t = DVE.put(lambda e: e.memset(nt[0][:], 0.0))
        ACT.put(lambda e: e.activation(nt[1][:], nt[0][:], AF.Sigmoid), t)
        DVE.put(lambda e: e.memset(ones[:], 1.0))
        DVE.put(lambda e: e.memset(Mac[:, 0, :], 0.0))
        DVE.put(lambda e: e.memset(Tx[:, E:E + 1], 1.0))
        t = DVE.put(lambda e: e.memset(zero[:], 0.0))
        T["zero"] = SP.dma(lambda e: e.dma_start(out[M:M + 128, :], zero[:]), d_z, t)

        def weave(*gens):
            wait, queue = 0, []
            for g in gens:
                if isinstance(g, int):
                    wait = g
                else:
                    queue.append([wait, g])
                    wait = 0
            while queue:
                for item in list(queue):
                    if item[0]:
                        item[0] -= 1
                    elif next(item[1], queue) is queue:
                        queue.remove(item)

        def make_first(c):
            w = slice(c * CW, c * CW + CW)
            t = ACT.put(lambda e: e.copy(Wh[:, 0, w], Wf[:, 0, w]), T["lw0", c], on=s_hi)
            T["lo0"] = POOL.put(lambda e: e.tensor_tensor(Wl[:, 0, w], Wf[:, 0, w], Wh[:, 0, w].bitcast(F32), ALU.subtract), t, on=s_lo)

        POOL.run(lambda e: None, T["mh"])
        weave(ln(0))
        weave(ln_bias(0))
        split_k(0)
        norm_q(0)
        low_q(0, 0)
        low_q(0, 1)
        split_v(0, False)
        split_v(0, True)
        ACT.put(lambda e: e.activation(tg[:], gg[:], AF.Tanh), T["gg"])
        T["tg"] = ACT.put(lambda e: e.activation(tn[:], gg[:], AF.Tanh, scale=-1.0))
        DVE.put(lambda e: e.tensor_copy(SUb[:], C[:, C_SU:C_SU + 128]), T["ld"])
        DVE.put(lambda e: e.tensor_copy(io16[:], iota(VT)))
        T["consts"] = T["mac", 0] = DVE.put(lambda e: e.tensor_copy(stepb[:], C[:, C_STEP:C_STEP + 1].broadcast_to((128, 128))))
        DVE.run(lambda e: None, T["ld2"], T["tg"])
        PE.run(lambda e: None, T["ld"], T["ld2"])
        POOL.run(lambda e: None, T["ld2"])
        on = lambda f, b: [f(b)] if 0 <= b < B else []
        for b in range(B + 1):
            attend, more = b < B, b + 1 < B
            if more:
                split_k(b + 1)
            if attend:
                for c in range(4):
                    qk(b, c)
                    score(b, c)
                    if c == 1 and more:
                        split_v(b + 1, False)
            weave(*on(choose, b - 2), *on(one_hots, b - 3), 6, *on(ln, b + 1), 9, *on(ffn_bias, b - 1),
                  6, *([low_scores(b)] if attend else []))
            if b >= 2:
                gate_sigmoids(b - 2)
                before(b - 2)
            if b >= 1:
                norm_t(b - 1, 0)
                norm_t(b - 1, 1)
            if more:
                split_v(b + 1, True)
            if b + 2 < B:
                load_k(b + 2)
                load_x(b + 2)
            weave(*on(ln_bias, b + 1), *on(gates, b - 2), *on(rank, b - 2))
            if more:
                norm_q(b + 1)
            if b < NCH:
                make_first(b)
            if b >= 2:
                store_rows(b - 2)
            if attend:
                av(b, 0)
                av(b, 1)
                if b + 2 < B:
                    load_v(b + 2)
                if b + 1 < NCH:
                    load_first(b + 1)
            else:
                landed(0)
                load_w(1, T["av", B - 1])
            if attend:
                add_x(b, 0)
            if more:
                low_q(b + 1, 0)
                low_q(b + 1, 1)
            if b >= 1:
                turn_t(b - 1, 0)
                turn_t(b - 1, 1)
            if b >= 3:
                table(b - 3)
            if b >= 1:
                out_base(b - 1)
                store_base(b - 1)
            if b >= 2:
                for q in POOL_HOTS:
                    one_hot(b - 2, q, POOL)
            if b >= 1:
                logits(b - 1)
            if attend:
                add_x(b, 1)
                weave(ffn_in(b))
        weave(choose(B - 1), one_hots(B - 2))
        before(B - 1)
        gate_sigmoids(B - 1)
        table(B - 2)
        weave(rank(B - 1))
        for q in POOL_HOTS:
            one_hot(B - 1, q, POOL)
        weave(one_hots(B - 1), gates(B - 1))
        store_rows(B - 1)
        table(B - 1)

        t = PE.put(lambda e: e.matmul(ps[6][:, 64:64 + E], ones[:], Mac[:, B, :], start=True, stop=True), T["mac", B])
        t = DVE.put(lambda e: e.tensor_scalar(Ni[:], ps[6][:, 64:64 + E], 127.0, None, op0=ALU.add), t)
        t = DVE.put(lambda e: e.tensor_scalar(Ti[:], Ni[:], 7, None, op0=ALU.arith_shift_right), t)
        t = DVE.put(lambda e: e.tensor_scalar(Tf[:], Ti[:], 1.0, None, op0=ALU.max), t)
        tf = t
        t = DVE.put(lambda e: e.tensor_tensor_scan(Ee[:], Tf[:], Tf[:], 0.0, ALU.add, ALU.bypass), t)
        te_ = t
        t = DVE.put(lambda e: e.tensor_tensor(Tx[:, 0:E], Ee[:], Tf[:], ALU.subtract), t)
        t = DVE.put(lambda e: e.tensor_tensor(us[:], C[:, C_SEL:C_SEL + 51].rearrange("p (c e) -> p c e", c=3),
                                             Tx[:].unsqueeze(1).broadcast_to((128, 3, E + 1)), ALU.mult), t)
        t = DVE.put(lambda e: e.tensor_reduce(uu[:], us[:], AX, ALU.add), t)
        for c in range(2):
            ts = DVE.put(lambda e, c=c: e.tensor_scalar(Sm[:, c, :], iota(NTP), uu[:, c:c + 1], None, op0=ALU.is_equal), t)
        tc = DVE.put(lambda e: e.tensor_scalar(cm[:], iota(NTP), uu[:, 2:3], None, op0=ALU.is_ge), t)

        p = ACT.put(lambda e: e.copy(tab[:], ps[7][:, 0:VT]), T["tb", B - 1])

        def mm(e):
            for c in range(2):
                m = e.transpose(ps[4][:, 128 * c:128 * c + 128], tab[:, 128 * c:128 * c + 128], idm)
            return m

        p = PE.put(mm, p, T["tTc", 0])
        p = ACT.put(lambda e: e.copy(tabT[:], ps[4][:, 0:256].rearrange("p (c t) -> p c t", c=2)), p)

        def mm(e):
            for c in range(2):
                m = e.matmul(ps[6][:, 0:NTP], tabT[:, c, :], Sm[:, c, :], start=(c == 0), stop=(c == 1))
            return m

        p = PE.put(mm, p, ts, tf, T[("prr",)], T[("lgr",)])
        T["src"] = DVE.put(lambda e: e.tensor_scalar(src[:], ps[6][:, 0:NTP], -1.0, 0.0, op0=ALU.add, op1=ALU.max), p)
        t = DVE.put(lambda e: e.tensor_scalar(iv[:], ps[6][:, 0:NTP], 0.0, C[:, C_PAD:C_PAD + 1], op0=ALU.is_equal, op1=ALU.mult), p)
        T["dst"] = DVE.put(lambda e: e.scalar_tensor_tensor(dst[:], ps[6][:, 0:NTP], -1.0, iv[:], ALU.add, ALU.add), t)

        def mm(e):
            e.matmul(ps[5][:, 0:NTP], ones[:], cm[:], start=True, stop=True)
            return e.matmul(ps[5][:, NTP:2 * NTP], stepb[:], cm[:], start=True, stop=True)

        p = PE.put(mm, tc, T["tTc", 1])
        DVE.put(lambda e: e.tensor_copy(te[:, 0:2, :], ps[5][:, 0:2 * NTP].rearrange("p (a t) -> p a t", a=2)), p)
        T["tabs"] = DVE.put(lambda e: e.tensor_scalar(te[:, 2, :], ps[5][:, 0:NTP], 4.0, 4.0, op0=ALU.mult, op1=ALU.add), p)
        T["ends"] = DVE.put(lambda e: e.tensor_copy(Ei[:], Ee[:]), te_)
        t = DVE.put(lambda e: e.tensor_tensor(ut[:], C[:, C_CNT:C_CNT + 32].rearrange("p (c e) -> p c e", c=2),
                                             Tf[:].unsqueeze(1).broadcast_to((128, 2, E)), ALU.mult), tf)
        t = DVE.put(lambda e: e.tensor_reduce(un[:], ut[:], AX, ALU.add), t)
        t = DVE.put(lambda e: e.tensor_copy(cntb[:], un[:].unsqueeze(2).broadcast_to((128, 2, 128))), t)

        def mm(e):
            e.matmul(ps[5][:, 160:160 + NTP], cntb[:, 0, :], cm[:], start=True, stop=True)
            return e.matmul(ps[5][:, 240:240 + NTP], cntb[:, 1, :], cm[:], start=True, stop=True)

        p = PE.put(mm, t)
        t = DVE.put(lambda e: e.tensor_tensor(j4[:], iota(NTP), ps[5][:, 160:160 + NTP], ALU.subtract), p)
        tn_ = DVE.put(lambda e: e.tensor_scalar(Tm[:], Tf[:, 0:1], -1.0, None, op0=ALU.add))
        tn_ = DVE.put(lambda e: e.tensor_scalar(iv[:], ps[5][:, 240:240 + NTP], Tm[:, 0:1], 1.0, op0=ALU.add, op1=ALU.max), p, T["dst"], tn_)
        t = DVE.put(lambda e: e.tensor_scalar(j4[:], j4[:], 4.0, None, op0=ALU.mult), t)
        for m_ in range(NCH):
            t = DVE.put(lambda e, m_=m_: e.scalar_tensor_tensor(fl[m_][:], iv[:], float(m_ + 1), j4[:], ALU.mult, ALU.is_le), t, tn_)
        for m_ in range(1, NCH):
            t = DVE.put(lambda e, m_=m_: e.tensor_tensor(fl[0][:], fl[0][:], fl[m_][:], ALU.add), t)
        t = DVE.put(lambda e: e.tensor_tensor(fl[0][:], fl[0][:], te[:, 2, :], ALU.add), t, T["tabs"])
        T["cp"] = DVE.put(lambda e: e.tensor_scalar(te[:, 3, :], fl[0][:], float(NCH * E), None, op0=ALU.min), t)

        def refill(e_):
            def w(e):
                v = e.value_load(Ei[0:1, e_ - 3:e_ - 2], min_val=1, max_val=NT)
                e.wait_ge(s_yb[0], v)
            SP.run(w, T["ends"])
            load_w(e_)

        def gather(t):
            w = was("tx", t - 4) + was("gc", t - 4) + ([T["src"], T["st_row", B - 1], T["st_row", B - 2]] if t < 4 else [])
            T["ga", t] = POOL.dma(lambda e: e.indirect_dma_start(
                xg[t % 4][:], None, rows, bass.IndirectOffsetOnAxis(src[:, t:t + 1], axis=0)), d_g[t % 4], *w)

        def scatter(t):
            w = was("sca", t - 1) if t else [T["dst"], T["st_base", B - 1], T["st_base", B - 2], T["zero"]]
            T["sca", t] = POOL.dma(lambda e: e.indirect_dma_start(
                out, bass.IndirectOffsetOnAxis(dst[:, t:t + 1], axis=0), ys[t % 3][:], None, compute_op=ALU.add), d_s, T["ys", t], *w)

        R = {}

        def slot(e, t, load=False):
            if load:
                R[e, t] = e.value_load(te[0:1, 1, t:t + 1], min_val=0, max_val=2)
            return R[e, t]

        PX, PA, PB_, PT, PY = ps[0], ps[1], ps[2], ps[3], ps[4]

        def chunks(e, t):
            g0 = e.value_load(te[0:1, 3, t:t + 1], min_val=NCH, max_val=NCH * E)
            g1 = e.value_load(te[0:1, 3, t + 1:t + 2], min_val=NCH, max_val=NCH * E)
            return g0, g1

        def place(g):
            return slice(None), bass.ds((g >> 2) % 3, 1), bass.ds((g % NCH) * CW, CW)

        ACT.run(lambda e: None, T["st_base", B - 1], T["st_row", B - 1], T["st_base", B - 2], T["st_row", B - 2], T["zero"])

        def make_hi(t):
            def f(e):
                g0, g1 = chunks(e, t)
                with e.If(g0 < g1):
                    with e.Fori(g0, g1) as g:
                        e.wait_ge(s_raw[0], e.snap((g >> 2) + 1))
                        w = place(g)
                        e.copy(Wh[w], Wf[w]).then_inc(s_hi[0], 1)
            ACT.run(f, T["cp"])

        def make_lo(t):
            def f(e):
                g0, g1 = chunks(e, t)
                with e.If(g0 < g1):
                    with e.Fori(g0, g1) as g:
                        e.wait_ge(s_hi[0], e.snap(g + 1))
                        w = place(g)
                        e.tensor_tensor(Wl[w], Wf[w], Wh[w].bitcast(F32), ALU.subtract).then_inc(s_lo[0], 1)
            POOL.run(f, T["cp"])

        def trans_x(t):
            i = t % 2

            def tr(e):
                for c in range(4):
                    m = e.transpose(PX[:, 128 * c:128 * c + 128], xg[t % 4][:, 128 * c:128 * c + 128], idm)
                return m
            T["tx", t] = PE.put(tr, T["ga", t], *(was("xTl", t - 1) if t else [T["sc", B - 1, 3]]))
            px = PX[:].rearrange("p (c t) -> p c t", c=4)
            k = ACT.put(lambda e: e.copy(xTh[i][:], px), T["tx", t], *was("l1b", t - 2))
            T["xTl", t] = DVE.put(lambda e: e.tensor_tensor(xTl[i][:], px, xTh[i][:].bitcast(F32), ALU.subtract), k)

        def gate(t):
            def gc(e):
                r = e.value_load(te[0:1, 0, t:t + 1], min_val=0, max_val=E - 1)
                return e.copy(gcol[t % 4][:], xg[t % 4][:, H:ROW][:, bass.ds(r, 1)])
            T["gc", t] = ACT.put(gc, T["ga", t], T["tabs"], *was("ys", t - 4))

        def product(e, P_, lh, r, col):
            n = 0
            for c in range(4):
                for xl, wl in PASSES:
                    at_ = CW * c + col
                    m = e.matmul(P_[:], lh[xl][:, c, :], (Wh, Wl)[wl][:, bass.ds(r, 1), at_:at_ + H], start=(n == 0), stop=(n == 11))
                    n += 1
            return m

        def l1(t, half):
            P_ = (PA, PB_)[half]

            def mm(e):
                if half == 0:
                    made = e.value_load(te[0:1, 2, t:t + 1], min_val=NCH, max_val=NCH * E)
                    slot(e, t, True)
                    e.wait_ge(s_lo[0], made)
                return product(e, P_, (xTh[t % 2], xTl[t % 2]), slot(e, t), H * half)
            T["l1" + "ab"[half], t] = PE.put(mm, T["xTl", t], T["tabs"], *was("h" + "ab"[half], t - 1))

        def act_a(t):
            def f(e):
                r = slot(e, t, True)
                return e.tensor_tensor(av_[:], PA[:], Bs[:, bass.ds(r, 1), 0:H], ALU.add)
            k = T["ha", t] = DVE.put(f, T["l1a", t], T["tabs"], *was("h", t - 1), *was("sg", t - 1))
            k = DVE.put(lambda e: e.tensor_scalar(av_[:], av_[:], LIMIT, None, op0=ALU.min), k)
            T["a", t] = k

        def sigm(t):
            T["sg", t] = ACT.put(lambda e: e.activation(sg[:], av_[:], AF.Sigmoid, scale=ALPHA), T["a", t], *was("h", t - 1))

        def act_b(t):
            k = T["hb", t] = DVE.put(lambda e: e.tensor_tensor(bv_[:], PB_[:], Bs[:, bass.ds(slot(e, t), 1), H:2 * H], ALU.add),
                                     T["l1b", t])
            k = DVE.put(lambda e: e.tensor_scalar(bv_[:], bv_[:], LIMIT, -LIMIT, op0=ALU.min, op1=ALU.max), k)
            k = DVE.put(lambda e: e.scalar_tensor_tensor(bv_[:], bv_[:], 1.0, av_[:], ALU.add, ALU.mult), k)
            T["h", t] = DVE.put(lambda e: e.tensor_tensor(hh[:], bv_[:], sg[:], ALU.mult), k, T["sg", t], *was("ta", t - 1))

        def trans_a(t):
            def tr(e):
                for c in range(4):
                    m = e.transpose(PT[:, 128 * c:128 * c + 128], hh[:, 128 * c:128 * c + 128], idm)
                return m
            T["ta", t] = PE.put(tr, T["h", t], *was("aTl", t - 1))
            pt = PT[:].rearrange("p (c t) -> p c t", c=4)
            k = ACT.put(lambda e: e.copy(aTh[:], pt), T["ta", t], *was("l2", t - 1))
            T["aTl", t] = DVE.put(lambda e: e.tensor_tensor(aTl[:], pt, aTh[:].bitcast(F32), ALU.subtract), k)

        def l2(t):
            T["l2", t] = PE.put(lambda e: product(e, PY, (aTh, aTl), slot(e, t, t + 1 in ENDS), 2 * H), T["aTl", t], *was("yb", t - 1))

        def out_y(t):
            y = ys[t % 3]
            T["yb", t] = DVE.put(lambda e: e.tensor_tensor(y[:], PY[:], Bs[:, bass.ds(slot(e, t, t + 1 in ENDS), 1), 2 * H:CW], ALU.add),
                                 T["l2", t], *was("sca", t - 3), on=s_yb)
            T["ys", t] = ACT.put(lambda e: e.activation(y[:], y[:], AF.Copy, scale=gcol[t % 4][:]), T["yb", t], T["gc", t])

        gather(0)
        gather(1)
        gather(2)
        landed(1)
        load_w(2, T["tb", B - 1], T["ga", 0], T["ga", 1], T["ga", 2])
        landed(2)
        for e_ in range(3, E):
            refill(e_)
            landed(e_)

        trans_x(0)
        gate(0)
        def start(t):
            l1(t, 0)
            act_a(t)
            if t >= 1:
                trans_a(t - 1)
            if t + 3 < NT:
                gather(t + 3)
            if t + 1 < NT:
                trans_x(t + 1)
                gate(t + 1)
            sigm(t)
            make_hi(t)
            make_lo(t)
            l1(t, 1)
            act_b(t)
            if t >= 1:
                l2(t - 1)
                out_y(t - 1)
                scatter(t - 1)

        def finish(t):
            trans_a(t - 1)
            l2(t - 1)
            out_y(t - 1)
            scatter(t - 1)
            POOL.run(lambda e: None, T["sca", t - 1], *[T["ga", u] for u in range(t, min(t + 3, NT))])

        tiles = (PE, ACT, DVE, POOL)

        def only(t, more):
            def cond(e):
                n = e.value_load(Ei[0:1, E - 1:E], min_val=1, max_val=NT)
                return n > t if more else n <= t
            for line in tiles:
                line.only(cond)

        def close(n=1):
            for line in tiles * n:
                line.close()

        for t in range(NT):
            if t in ENDS:
                kept = [(line.n, dict(line.seen)) for line in tiles], [c[1] for c in chans], dict(T)
                only(t, False)
                finish(t)
                close()
                for line, (n, seen) in zip(tiles, kept[0]):
                    line.n, line.seen = n, seen
                for c, n in zip(chans, kept[1]):
                    c[1] = n
                T.clear()
                T.update(kept[2])
                if t != ENDS[0]:
                    close()
                only(t, True)
            start(t)
        finish(NT)
        close()

        block = es.enter_context(nc.Block())

        @block.sync
        def _(e):
            SP.emit(e)

        @block.scalar
        def _(e):
            ACT.emit(e)

        @block.gpsimd
        def _(e):
            POOL.emit(e)

        @block.vector
        def _(e):
            DVE.emit(e)

        @block.tensor
        def _(e):
            PE.emit(e)


def lay_out(x, ctx_2048, g_xattn, g_ffn, L0_ffn_norm_w, L0_ffn_gate_w, L0_ffn_gate_b, L0_ffn_w1, L0_ffn_b1, L0_ffn_w2, L0_ffn_b2):
    f = lambda a: np.asarray(a)
    w1 = f(L0_ffn_w1).reshape(E, H, 2, 4, 128)
    w2 = f(L0_ffn_w2).reshape(E, H, 4, 128)
    wts = np.empty((E, 128, 4, 3, H), np.float32)
    wts[:, :, :, 0:2] = w1.transpose(0, 4, 3, 2, 1)
    wts[:, :, :, 2] = w2.transpose(0, 3, 2, 1)
    b1 = f(L0_ffn_b1).reshape(E, H, 2)
    bias = np.concatenate([b1[:, :, 0], b1[:, :, 1], f(L0_ffn_b2)], axis=1)
    ctxT = f(ctx_2048).transpose(0, 2, 1).reshape(B, 4, 128, S).transpose(0, 2, 1, 3)
    gw = f(L0_ffn_gate_w).reshape(E, 4, 128).transpose(2, 1, 0)
    return dict(x=f(x).reshape(M, H), ctx=f(ctx_2048), ctxT=ctxT, gx=f(g_xattn), gf=f(g_ffn), nw=f(L0_ffn_norm_w), gw=gw,
                gb=f(L0_ffn_gate_b), wts=wts.reshape(E, 128, WS), bias=bias, cst=shape_constants())


def kernel(**inputs):
    import concourse.bacc as _bacc
    from concourse.bass_utils import run_bass_kernel_spmd as _run

    nc = _bacc.Bacc("TRN2", target_bir_lowering=False, num_devices=1)
    arrays, args = {}, {}
    for name, a in lay_out(**inputs).items():
        a = np.ascontiguousarray(a)
        arrays[f"in_{name}"] = a
        args[name] = nc.dram_tensor(f"in_{name}", a.shape, mybir.dt.from_np(a.dtype), kind="ExternalInput").ap()
    args["out"] = nc.dram_tensor("out_0", (M + 128, H), F32, kind="ExternalOutput").ap()
    build(nc, **args)
    r = _run(nc, [arrays], core_ids=[0])
    return r.results[0]["out_0"][:M].reshape(B, S, H)
```
